# Optimizing a Trainium2 kernel written in Bass

```python
import numpy as np
import jax
import jax.numpy as jnp

def _softmax(x, axis=-1):
    return jax.nn.softmax(x, axis=axis)

def _gelu(x):
    return jax.nn.gelu(x, approximate=True)

def _silu(x):
    return jax.nn.silu(x)

def _sigmoid(x):
    return jax.nn.sigmoid(x)

def _layernorm(x, axis=-1, eps=1e-05):
    m = jnp.mean(x, axis=axis, keepdims=True)
    v = jnp.var(x, axis=axis, keepdims=True)
    return (x - m) / jnp.sqrt(v + eps)

def _scatter_add(tgt, idx, src, axis=0):
    return tgt.at[idx].add(src)

def _segment_sum(src, seg, n):
    return jax.ops.segment_sum(src, seg, n)
kernel_name = 'mk_macaron_d1_jaxref_r8_1a7ed7'

def setup_inputs(seed: int=0):
    np.random.seed(seed)
    _w = jnp.asarray

    def _L0_attn_setup():
        import jax, jax.numpy as jnp
        import numpy as np
        import math
        H = 16
        NH = 4
        CHUNK = 128
        WIN = 128
        ROPE_THETA = 500000.0
        BASE_LR_INV = 0.001 + math.log(-math.expm1(-0.001))

        def rmsnorm(x, w, eps=1e-06):
            return x * jax.lax.rsqrt(jnp.mean(x * x, axis=-1, keepdims=True) + eps) * w

        def rope(x, cos, sin):
            d2 = x.shape[-1] // 2
            x1, x2 = (x[..., :d2], x[..., d2:])
            c = cos[None, :, None, :]
            s_ = sin[None, :, None, :]
            return jnp.concatenate([x1 * c - x2 * s_, x2 * c + x1 * s_], axis=-1)
        key = jax.random.key(seed)
        b, s, d = (2, 256, 256)
        fd = d // NH
        dh = fd
        ks = jax.random.split(key, 12)
        return {'hidden_states': jax.random.normal(ks[0], (b, s, d), jnp.float32), 'Wqkv': jax.random.normal(ks[1], (3 * d, d), jnp.float32) / math.sqrt(d), 'Wo': jax.random.normal(ks[2], (d, d), jnp.float32) / math.sqrt(d), 'q_norm_w': jnp.ones((d,), jnp.float32), 'k_norm_w': jnp.ones((d,), jnp.float32), 'w0': jax.random.normal(ks[3], (NH, dh, fd), jnp.float32) / math.sqrt(fd), 'w1': jax.random.normal(ks[4], (NH, fd, dh), jnp.float32) / math.sqrt(dh), 'w2': jax.random.normal(ks[5], (NH, dh, fd), jnp.float32) / math.sqrt(fd), 'lr_w': jax.random.normal(ks[6], (3 * NH, d), jnp.float32) * 0.02, 'lr_b': jnp.zeros((3 * NH,), jnp.float32), 'qk_scale': jnp.ones((d, 2), jnp.float32), 'qk_offset': jnp.zeros((d, 2), jnp.float32), 'ttt_norm_w': jnp.ones((fd,), jnp.float32)}
    _L0_attn_in = _L0_attn_setup()

    def _L0_ffn_setup():
        import jax, jax.numpy as jnp
        import numpy as np
        E, H, I, TOPK = (16, 256, 176, 4)
        B, S = (2, 128)
        key = jax.random.key(seed)
        ks = jax.random.split(key, 6)
        hidden_states = jax.random.normal(ks[0], (B, S, H), dtype=jnp.float32)
        topk_idx = jax.random.randint(ks[1], (B, S, TOPK), 0, E)
        topk_weight = jax.random.uniform(ks[2], (B, S, TOPK), dtype=jnp.float32) / TOPK
        gate_weight = jax.random.normal(ks[3], (E, I, H), dtype=jnp.float32) * (1.0 / np.sqrt(H))
        up_weight = jax.random.normal(ks[4], (E, I, H), dtype=jnp.float32) * (1.0 / np.sqrt(H))
        down_weight = jax.random.normal(ks[5], (E, H, I), dtype=jnp.float32) * (1.0 / np.sqrt(I))
        return {'hidden_states': hidden_states, 'topk_idx': topk_idx, 'topk_weight': topk_weight, 'gate_weight': gate_weight, 'up_weight': up_weight, 'down_weight': down_weight}
    _L0_ffn_in = _L0_ffn_setup()
    _d = {'L0_attn_hidden_states': _L0_attn_in['hidden_states'], 'L0_attn_Wqkv': _L0_attn_in['Wqkv'], 'L0_attn_Wo': _L0_attn_in['Wo'], 'L0_attn_q_norm_w': _L0_attn_in['q_norm_w'], 'L0_attn_k_norm_w': _L0_attn_in['k_norm_w'], 'L0_attn_w0': _L0_attn_in['w0'], 'L0_attn_w1': _L0_attn_in['w1'], 'L0_attn_w2': _L0_attn_in['w2'], 'L0_attn_lr_w': _L0_attn_in['lr_w'], 'L0_attn_lr_b': _L0_attn_in['lr_b'], 'L0_attn_qk_scale': _L0_attn_in['qk_scale'], 'L0_attn_qk_offset': _L0_attn_in['qk_offset'], 'L0_attn_ttt_norm_w': _L0_attn_in['ttt_norm_w'], 'L0_ffn_topk_idx': _L0_ffn_in['topk_idx'], 'L0_ffn_topk_weight': _L0_ffn_in['topk_weight'], 'L0_ffn_gate_weight': _L0_ffn_in['gate_weight'], 'L0_ffn_up_weight': _L0_ffn_in['up_weight'], 'L0_ffn_down_weight': _L0_ffn_in['down_weight']}
    _x0 = _d['L0_attn_hidden_states']
    _d['L0_attn_hidden_states'] = jax.random.normal(jax.random.fold_in(jax.random.key(seed), 1), (4, 256, 256), dtype=_x0.dtype)
    del _x0
    return _d

def reference(L0_attn_hidden_states, L0_attn_Wqkv, L0_attn_Wo, L0_attn_q_norm_w, L0_attn_k_norm_w, L0_attn_w0, L0_attn_w1, L0_attn_w2, L0_attn_lr_w, L0_attn_lr_b, L0_attn_qk_scale, L0_attn_qk_offset, L0_attn_ttt_norm_w, L0_ffn_topk_idx, L0_ffn_topk_weight, L0_ffn_gate_weight, L0_ffn_up_weight, L0_ffn_down_weight):

    def _L0_attn_ref(hidden_states, Wqkv, Wo, q_norm_w, k_norm_w, w0, w1, w2, lr_w, lr_b, qk_scale, qk_offset, ttt_norm_w):
        import jax, jax.numpy as jnp
        import numpy as np
        import math
        H = 16
        NH = 4
        CHUNK = 128
        WIN = 128
        ROPE_THETA = 500000.0
        BASE_LR_INV = 0.001 + math.log(-math.expm1(-0.001))

        def rmsnorm(x, w, eps=1e-06):
            return x * jax.lax.rsqrt(jnp.mean(x * x, axis=-1, keepdims=True) + eps) * w

        def rope(x, cos, sin):
            d2 = x.shape[-1] // 2
            x1, x2 = (x[..., :d2], x[..., d2:])
            c = cos[None, :, None, :]
            s_ = sin[None, :, None, :]
            return jnp.concatenate([x1 * c - x2 * s_, x2 * c + x1 * s_], axis=-1)
        b, s, d = hidden_states.shape
        hd = d // H
        fd = d // NH
        qkv = hidden_states @ Wqkv.T
        q, k, v = jnp.split(qkv, 3, axis=-1)
        aq = rmsnorm(q, q_norm_w).reshape(b, s, H, hd)
        ak = rmsnorm(k, k_norm_w).reshape(b, s, H, hd)
        av = v.reshape(b, s, H, hd)
        inv_freq = 1.0 / ROPE_THETA ** (jnp.arange(0, hd, 2, dtype=jnp.float32) / hd)
        ang = jnp.arange(s, dtype=jnp.float32)[:, None] * inv_freq[None, :]
        cos, sin = (jnp.cos(ang), jnp.sin(ang))
        aq = rope(aq, cos, sin)
        ak = rope(ak, cos, sin)
        scores = jnp.einsum('bqhd,bkhd->bhqk', aq, ak) / math.sqrt(hd)
        i = jnp.arange(s)[:, None]
        j = jnp.arange(s)[None, :]
        mask = (j <= i) & (i - j < WIN)
        scores = jnp.where(mask[None, None], scores, -jnp.inf)
        p = jax.nn.softmax(scores, axis=-1)
        attn_out = jnp.einsum('bhqk,bkhd->bqhd', p, av).reshape(b, s, d)
        fq = jax.nn.silu(q) * qk_scale[:, 0] + qk_offset[:, 0]
        fk = jax.nn.silu(k) * qk_scale[:, 1] + qk_offset[:, 1]
        fv = jax.nn.silu(v)
        fq = fq.reshape(b, s, NH, fd)
        fk = fk.reshape(b, s, NH, fd)
        fv = fv.reshape(b, s, NH, fd)
        fq = fq / (jnp.linalg.norm(fq, axis=-1, keepdims=True) + 1e-12)
        fk = fk / (jnp.linalg.norm(fk, axis=-1, keepdims=True) + 1e-12)
        lr = jax.nn.softplus(hidden_states @ lr_w.T + lr_b + BASE_LR_INV)
        lr0, lr1, lr2 = jnp.split(lr, 3, axis=-1)
        nC = s // CHUNK
        BH = b * NH

        def to_chunks(x):
            return x.transpose(0, 2, 1, 3).reshape(BH, nC, CHUNK, x.shape[-1]).transpose(1, 0, 2, 3)

        def lr_chunks(x):
            return x.transpose(0, 2, 1).reshape(BH, nC, CHUNK, 1).transpose(1, 0, 2, 3)
        qc, kc, vc = (to_chunks(fq), to_chunks(fk), to_chunks(fv))
        l0, l1, l2 = (lr_chunks(lr0), lr_chunks(lr1), lr_chunks(lr2))
        w0b = jnp.tile(w0, (b, 1, 1))
        w1b = jnp.tile(w1, (b, 1, 1))
        w2b = jnp.tile(w2, (b, 1, 1))

        def step(carry, xs):
            w0c, w1c, w2c = carry
            qi, ki, vi, li0, li1, li2 = xs
            gate = jnp.einsum('bcd,bhd->bch', ki, w0c)
            hpre = jnp.einsum('bcd,bhd->bch', ki, w2c)
            hid = jax.nn.silu(gate) * hpre
            dh_ = jnp.einsum('bco,boh->bch', vi, w1c)
            dhpre = dh_ * jax.nn.silu(gate)
            sig = jax.nn.sigmoid(gate)
            dgate = dh_ * hpre * (sig * (1.0 + gate * (1.0 - sig)))
            w0n = w0c + jnp.einsum('bch,bcd->bhd', dgate * li0, ki)
            w2n = w2c + jnp.einsum('bch,bcd->bhd', dhpre * li2, ki)
            w1n = w1c + jnp.einsum('bco,bch->boh', vi * li1, hid)
            gq = jnp.einsum('bcd,bhd->bch', qi, w0n)
            hq = jax.nn.silu(gq) * jnp.einsum('bcd,bhd->bch', qi, w2n)
            oi = jnp.einsum('bch,boh->bco', hq, w1n)
            return ((w0n, w1n, w2n), oi)
        _, out_c = jax.lax.scan(step, (w0b, w1b, w2b), (qc, kc, vc, l0, l1, l2))
        ttt = out_c.transpose(1, 0, 2, 3).reshape(b, NH, s, fd).transpose(0, 2, 1, 3)
        ttt = rmsnorm(ttt, ttt_norm_w).reshape(b, s, d)
        return (attn_out + ttt) @ Wo.T

    def _L0_ffn_ref(hidden_states, topk_idx, topk_weight, gate_weight, up_weight, down_weight):
        import jax, jax.numpy as jnp
        import numpy as np
        E, H, I, TOPK = (16, 256, 176, 4)
        B, S = (2, 128)
        b, s, h = hidden_states.shape
        n_tokens = b * s
        topk = topk_idx.shape[-1]
        x = hidden_states.reshape(n_tokens, h)
        flat_expert = topk_idx.reshape(-1)
        flat_weight = topk_weight.reshape(-1).astype(hidden_states.dtype)
        perm = jnp.argsort(flat_expert)
        tok = jnp.repeat(jnp.arange(n_tokens), topk)[perm]
        xs = x[tok]
        group_sizes = jnp.bincount(flat_expert, length=E).astype(jnp.int32)
        gate = jax.lax.ragged_dot(xs, jnp.swapaxes(gate_weight, 1, 2), group_sizes)
        up = jax.lax.ragged_dot(xs, jnp.swapaxes(up_weight, 1, 2), group_sizes)
        h_act = jax.nn.silu(gate) * up
        down = jax.lax.ragged_dot(h_act, jnp.swapaxes(down_weight, 1, 2), group_sizes)
        w_sorted = flat_weight[perm]
        out = jnp.zeros((n_tokens, h), hidden_states.dtype).at[tok].add(down * w_sorted[:, None])
        return out.reshape(b, s, h)
    x = L0_attn_hidden_states
    x = x + 0.5 * _L0_ffn_ref(_layernorm(x, axis=-1), L0_ffn_topk_idx, L0_ffn_topk_weight, L0_ffn_gate_weight, L0_ffn_up_weight, L0_ffn_down_weight)
    x = x + _L0_attn_ref(_layernorm(x, axis=-1), L0_attn_Wqkv, L0_attn_Wo, L0_attn_q_norm_w, L0_attn_k_norm_w, L0_attn_w0, L0_attn_w1, L0_attn_w2, L0_attn_lr_w, L0_attn_lr_b, L0_attn_qk_scale, L0_attn_qk_offset, L0_attn_ttt_norm_w)
    x = x + 0.5 * _L0_ffn_ref(_layernorm(x, axis=-1), L0_ffn_topk_idx, L0_ffn_topk_weight, L0_ffn_gate_weight, L0_ffn_up_weight, L0_ffn_down_weight)
    return x

_drawn_inputs = setup_inputs


def setup_inputs(seed=0):
    import zlib

    import numpy as np

    out = dict(_drawn_inputs(seed))
    spreads = {'L0_attn_q_norm_w': (1.0, 0.2),
     'L0_attn_k_norm_w': (1.0, 0.2),
     'L0_attn_lr_b': (0.0, 0.8),
     'L0_attn_qk_scale': (1.0, 0.2),
     'L0_attn_qk_offset': (0.0, 0.1),
     'L0_attn_ttt_norm_w': (1.0, 0.2)}
    factors = {'L0_attn_lr_w': 8.0}
    for name, (base, spread) in spreads.items():
        noise = np.random.default_rng([zlib.crc32(name.encode()), seed]).standard_normal(out[name].shape)
        drawn = base * np.exp(spread * noise) if base else spread * noise
        out[name] = jnp.asarray(drawn.astype(out[name].dtype))
    for name, factor in factors.items():
        out[name] = (out[name] * factor).astype(out[name].dtype)
    return out
```

```python
import math
from contextlib import ExitStack

import concourse.bass as bass
from concourse import mybir

F32 = mybir.dt.float32
BF16 = mybir.dt.bfloat16
I32 = mybir.dt.int32
ALU = mybir.AluOpType
ACT = mybir.ActivationFunctionType
AX = mybir.AxisListType

P = 128
B, S, D = 4, 256, 256
H, HD = 16, 16
NH, FD = 4, 64
E, I, TOPK = 16, 176, 4
DK = D // P
FT = E * I // P
NPAIR = NH // 2
VPAD = 16
NPAR = 6 * D + FD + 3 * NH
MASKED = -1.0e30
BASE_LR_INV = 0.001 + math.log(-math.expm1(-0.001))
ORDER = [(1, 0), (1, 1), (2, 0), (0, 0), (2, 1), (0, 1), (3, 0), (3, 1)]
NT = len(ORDER)


def unit_heads(t, u):
    return [2 * u, 2 * u + 1, 8 + 2 * u, 9 + 2 * u] if t == 0 else [2 * u, 2 * u + 1]


KV_SLOT = {1: 0, 2: 1, 0: 0, 3: 1}
UNITS = [4 if t == 0 else 8 for _, t in ORDER]
UBASE = [sum(UNITS[:n]) for n in range(NT + 1)]


def schedule():
    ffn = [[("G", f), ("G1", f)] + sum(
        ([("F", f, i)] + ([("D", f, i - 1)] if i else []) for i in range(FT)), [])
        + [("D", f, FT - 1), ("FE", f)] for f in range(2)]
    steps = [("L", 0), ("G", 0), ("P1", 0), ("G1", 0), ("P2", 0), ("C",), ("N", 0), ("N2", 0)]
    ffn1, ffn2 = ffn[0][2:], ffn[1]
    steps += ffn1[:8]
    ffn1 = ffn1[8:]
    steps += [("P3", 0), ("P4", 0)]
    for n in range(NT + 1):
        last, here, nxt = n - 1 >= 0, n < NT, n + 1 < NT
        misc = ([("L", n + 1)] if nxt else []) + ([("O0", n - 1), ("O1", n - 1)] if last else []) + ([("P1", n + 1)] if nxt else []) \
            + ([("Ta", n)] if here else []) + ([("O2", n - 1)] if last else []) \
            + ([("P2", n + 1)] if nxt else []) + ([("O3", n - 1)] if last else []) \
            + ([("Tb", n)] if here else []) + ([("N", n + 1)] if nxt else []) \
            + ([("Tc1", n)] if here else []) + ([("N2", n + 1), ("P3", n + 1)] if nxt else []) \
            + ([("Tc2", n)] if here else []) + ([("P4", n + 1)] if nxt else []) \
            + ([("Tc3", n)] if here else [])
        fill = []
        if n < 2:
            k = len(ffn1) // 3 if n == 0 else len(ffn1)
            fill, ffn1 = ffn1[:k], ffn1[k:]
        if n == 6:
            at = misc.index(("O3", n - 1)) + 1
            fill = [None] * 22 + ffn2[:14]
            ffn2 = ffn2[14:]
        if n == 7:
            fill, ffn2 = ffn2[:24], ffn2[24:]
        if n == 8:
            fill, ffn2 = ffn2, []
        units = UNITS[n] if here else 1
        slots = []
        for u in range(units):
            slots.append([])
        out = []
        for u in range(units):
            a = misc[len(misc) * u // units:len(misc) * (u + 1) // units]
            f = [x for x in fill[len(fill) * u // units:len(fill) * (u + 1) // units] if x]
            mix = []
            while a or f:
                if a:
                    mix.append(a.pop(0))
                if f:
                    mix.append(f.pop(0))
                if len(f) > len(a):
                    mix.append(f.pop(0))
            if here:
                half = len(mix) // 2
                out += [("S", n, u)] + mix[:half] + [("T", n, u)] + mix[half:] + [("V", n, u)]
            else:
                out += mix
        steps += out
    return steps


SCHEDULE = schedule()


def build(nc, x_d, wff_d, wqkv_d, wo_d, w02_d, w1_d, idx_d, topw_d, par_d, ident_d, mask_d, small_d, expand_d,
          out_d):
    ctx = ExitStack()
    with ctx:
        def sb(name, shape, dt=F32):
            return ctx.enter_context(nc.sbuf_tensor(name, shape, dt))

        def bank(name, dt=F32, n=512):
            return ctx.enter_context(nc.psum_tensor(name, [P, n], dt))

        def sem(name):
            return ctx.enter_context(nc.semaphore(name))

        wff = sb("wff", [P, FT, 3 * D])
        wqkv = sb("wqkv", [P, DK, 3 * D + 3 * NH])
        wo = sb("wo", [P, DK, D])
        par = sb("par", [P, NPAR])
        ident = sb("ident", [P, P])
        maskf = sb("maskf", [P, 3 * P])
        small = sb("small", [P, 48 + 2 + E])
        identb = sb("identb", [P, P], BF16)
        mask = sb("mask", [P, 3 * P], BF16)
        cosw = sb("cosw", [P, 2, 512])
        sinw = sb("sinw", [P, 2, 512])
        halfc = sb("halfc", [P, 16])
        w02 = sb("w02", [P, 3, NPAIR, 2, 2 * FD])
        w1oh = sb("w1oh", [P, 3, NPAIR, 2 * FD])
        w1ho = sb("w1ho", [P, 3, NPAIR, 2 * FD])
        INIT = 2
        trig = small[:, 0:48].rearrange("p (t k d) -> p t k d", t=2, k=3)
        head_mask = small[:, 48:50]
        expert_no = small[:, 50:50 + E]
        xs = sb("xs", [P, B, 2, D])
        idx_i = sb("idx_i", [P, 2, TOPK], I32)
        idx_f = sb("idx_f", [P, 2, TOPK])
        topw = sb("topw", [P, 2, TOPK])
        coef1 = sb("coef1", [P, 2, TOPK, E])
        coef = sb("coef", [P, 2, E])
        coef_r = sb("coef_r", [P, 2, 2, E])
        coef3 = sb("coef3", [P, 2, 3 * E], BF16)
        coefT = sb("coefT", [3 * E, 2 * P], BF16)
        coefx = sb("coefx", [P, FT, 2 * P])
        fst = sb("fst", [P, 2, 6])
        fmv = sb("fmv", [P, 2, 2])
        fve = sb("fve", [P, 2])
        frs = sb("frs", [P, 2])
        fxT = sb("fxT", [P, DK, 2 * P])
        fth = sb("fth", [P, 2, D])
        fa = sb("fa", [P, D])
        fb = sb("fb", [P, 2, D])
        fxn = fb
        fh = sb("fh", [P, 3, D])
        lst = sb("lst", [P, 2, 6])
        lmv = sb("lmv", [P, 2, 2])
        lve = sb("lve", [P, 2])
        lrs = sb("lrs", [P, 2])
        xn = sb("xn", [P, D])
        xnT = sb("xnT", [P, DK, P])
        ssqk = sb("ssqk", [P, 2, 2])
        msqk = sb("msqk", [P, 2, 2])
        rqk = sb("rqk", [P, 2, 2])
        th = sb("th", [P, 3 * D])
        qks = sb("qks", [P, 2 * D])
        rp1 = sb("rp1", [P, 2 * D])
        rp2 = th[:, 0:2 * D]
        rope = qks
        s2 = sb("s2", [P, 2 * D])
        s2v = sb("s2v", [P, 2, D])
        f1 = rp1
        f2 = sb("f2", [P, 2 * D])
        sqs = sb("sqs", [P, 2 * D])
        sqf = sqs
        ss8 = sb("ss8", [P, 2 * NH])
        nrm = sb("nrm", [P, 2 * NH])
        inv8 = sb("inv8", [P, 3, 2 * NH])
        fn = sb("fn", [P, 2 * D])
        fT = sb("fT", [P, 4, P])
        fvT = sb("fvT", [P, NPAIR, P])
        z = sb("z", [P, 5, 3 * NH])
        ez = sb("ez", [P, 3 * NH])
        rz = sb("rz", [P, 3 * NH])
        lz = sb("lz", [P, 24, 3 * NH])
        lr = sb("lr", [P, 2, 3 * NH])
        lrh = sb("lrh", [P, 2, NH])
        qTm = sb("qTm", [P, 2, 2, 2, P])
        kT = sb("kT", [P, 2, 2, 2 * P])
        vS = sb("vS", [P, 2, 2, D + VPAD])
        nmax = sb("nmax", [P, 2, 4])
        pST = sb("pST", [P, 4, 512])
        pS, pT = pST[:, 0:2], pST[:, 2:4]
        expand = pST[:].rearrange("p a b -> p (a b)").bitcast(BF16)[0:3 * E, 0:FT * P]
        rsum = sb("rsum", [P, 2, H])
        rinv = sb("rinv", [P, H])
        oS = sb("oS", [P, 512])
        aS = sb("aS", [P, D])
        ta = sb("ta", [P, D])
        si = sb("si", [P, D])
        hid = sb("hid", [P, D])
        dhp = sb("dhp", [P, D])
        q1 = sb("q1", [P, D])
        dg = sb("dg", [P, D])
        dd = sb("dd", [P, NPAIR, 2, 2 * FD])
        vl = sb("vl", [P, D])
        sg, tq, sq2, tg, q3 = ta, ta, si, q1, q1
        hqT = sb("hqT", [P, NPAIR, P])
        sqo = sb("sqo", [P, D])
        ss4 = sb("ss4", [P, NH])
        ms4 = sb("ms4", [P, NH])
        r4 = sb("r4", [P, NH])
        tt = sb("tt", [P, D])
        ttw, yS = tt, tt
        yT = sb("yT", [P, DK, P])
        GU = [bank("GU0"), bank("GU1")]
        DN = bank("DN")
        SC = bank("SC")
        PT = bank("PT")
        OT = bank("OT")
        X = bank("X")
        Y = bank("Y")

        qknw, scl, off = par[:, 0:512], par[:, 512:1024], par[:, 1024:1536]
        ttw_w, lrb = par[:, 1536:1536 + FD], par[:, 1536 + FD:NPAR]

        l_x = [sem(f"l_x{b}") for b in range(B)]
        l_route, l_par, l_small, l_ident, l_mask = (sem(n) for n in ("l_route", "l_par", "l_small", "l_ident", "l_mask"))
        l_wqkv, l_wo, l_expand, l_init = (sem(n) for n in ("l_wqkv", "l_wo", "l_expand", "l_init"))
        l_wff = [sem(f"l_wff{i}") for i in range(FT // 2)]
        stored = sem("stored")
        zeroed, consts, masks_ready, trig_ready = sem("zeroed"), sem("consts"), sem("masks_ready"), sem("trig_ready")
        coef_ready, coefT_psum, coefT_ready, coefx_psum, coefx_ready = (
            sem(n) for n in ("coef_ready", "coefT_psum", "coefT_ready", "coefx_psum", "coefx_ready"))
        dve_chain, act_chain, pool_chain = sem("dve_chain"), sem("act_chain"), sem("pool_chain")
        fstats, frstd, fxn_ready, fxT_psum, fxT_ready = (sem(n) for n in ("fstats", "frstd", "fxn_ready", "fxT_psum", "fxT_ready"))
        gu_ready, fth_ready, gated, h_ready, down_done, ffn_added = (
            sem(n) for n in ("gu_ready", "fth_ready", "gated", "h_ready", "down_done", "ffn_added"))
        ln_stats, ln_rstd, xn_ready, xnT_psum, xnT_ready, qkv_ready = (
            sem(n) for n in ("ln_stats", "ln_rstd", "xn_ready", "xnT_psum", "xnT_ready", "qkv_ready"))
        ss_ready, rqk_ready, th_ready, silu_ready, qk_scaled, qkv_sb, ez_ready, rz_ready, lr_ready = (
            sem(n) for n in ("ss_ready", "rqk_ready", "th_ready", "silu_ready", "qk_scaled", "qkv_sb", "ez_ready",
                             "rz_ready", "lr_ready"))
        f_ready, rope_ready, sqf_ready, ss8_ready, nrm_ready, fn_ready = (
            sem(n) for n in ("f_ready", "rope_ready", "sqf_ready", "ss8_ready", "nrm_ready", "fn_ready"))
        fT_psum, qkT_psum, fT_ready, qkT_ready, fvT_psum, fvT_ready = (
            sem(n) for n in ("fT_psum", "qkT_psum", "fT_ready", "qkT_ready", "fvT_psum", "fvT_ready"))
        scores_ready, nmax_ready, exp_done, pT_psum, pT_ready, pv_done = (
            sem(n) for n in ("scores_ready", "nmax_ready", "exp_done", "pT_psum", "pT_ready", "pv_done"))
        oS_ready, o_psum, attn_ready, y_ready, yT_psum, yT_ready, wo_psum, x2_ready = (
            sem(n) for n in ("oS_ready", "o_psum", "attn_ready", "y_ready", "yT_psum", "yT_ready", "wo_psum", "x2_ready"))
        ta_psum, ta_ready, grads_ready, dd_ready, tb_psum, w_updated = (
            sem(n) for n in ("ta_psum", "ta_ready", "grads_ready", "dd_ready", "tb_psum", "w_updated"))
        gq_psum, tq_ready, hq_ready, oi_psum, sqo_ready, ss4_ready, r4_ready, tt_ready, ttw_ready = (
            sem(n) for n in ("gq_psum", "tq_ready", "hq_ready", "oi_psum", "sqo_ready", "ss4_ready", "r4_ready",
                             "tt_ready", "ttw_ready"))

        def heads(ap, n, w):
            return ap.rearrange("p (n w) -> p n w", n=n, w=w)

        def spread(ap, n, w):
            return ap.unsqueeze(2).broadcast_to([P, n, w])

        def w_old(n):
            b, t = ORDER[n]
            return INIT if t == 0 else KV_SLOT[b]

        block = ctx.enter_context(nc.Block())

        @block.sync
        def _(sp):
            sp.dma_start(xs[:, 1], x_d[1].rearrange("(t p) d -> p t d", p=P)).then_inc(l_x[1], 16)
            sp.dma_start(ident[:], ident_d).then_inc(l_ident, 16)
            sp.dma_start(xs[:, 0], x_d[0].rearrange("(t p) d -> p t d", p=P)).then_inc(l_x[0], 16)
            sp.dma_start(wqkv[:], wqkv_d).then_inc(l_wqkv, 16)
            sp.dma_start(par[:], par_d.partition_broadcast(P)).then_inc(l_par, 16)
            sp.dma_start(small[:], small_d).then_inc(l_small, 16)
            sp.dma_start(idx_i[:], idx_d).then_inc(l_route, 16)
            sp.dma_start(topw[:], topw_d).then_inc(l_route, 16)
            sp.dma_start(expand, expand_d.bitcast(BF16)).then_inc(l_expand, 16)
            sp.dma_start(wff[:, 0:2, :], wff_d[:, 0:2, :]).then_inc(l_wff[0], 16)
            sp.dma_start(maskf[:], mask_d).then_inc(l_mask, 16)
            sp.wait_ge(zeroed, 3)
            for h in range(NH):
                p, a = h // 2, h % 2
                rows = slice(FD * a, FD * a + FD)
                sp.dma_start(w02[rows, INIT, p, :, FD * a:FD * a + FD], w02_d[h]).then_inc(l_init, 16)
                sp.dma_start(w1oh[rows, INIT, p, FD * a:FD * a + FD], w1_d[h, 0]).then_inc(l_init, 16)
                sp.dma_start(w1ho[rows, INIT, p, FD * a:FD * a + FD], w1_d[h, 1]).then_inc(l_init, 16)
            for i in range(1, FT // 2):
                sp.dma_start(wff[:, 2 * i:2 * i + 2, :], wff_d[:, 2 * i:2 * i + 2, :]).then_inc(l_wff[i], 16)
                if i == 2:
                    sp.dma_start(wo[:], wo_d).then_inc(l_wo, 16)
                    for b in (2, 3):
                        sp.dma_start(xs[:, b], x_d[b].rearrange("(t p) d -> p t d", p=P)).then_inc(l_x[b], 16)
            for n, (b, t) in enumerate(ORDER):
                if b:
                    sp.wait_ge(x2_ready, n + 1)
                    sp.dma_start(out_d[b, t * P:(t + 1) * P, :], xs[:, b, t]).then_inc(stored, 16)
            sp.wait_ge(ffn_added, 2)
            sp.dma_start(out_d[0].rearrange("(t p) d -> p t d", p=P), xs[:, 0]).then_inc(stored, 16)
            sp.wait_ge(stored, 16 * 7)

        @block.gpsimd
        def _(pool):
            links = [0]

            def link(ins):
                links[0] += 1
                ins.then_inc(pool_chain, 1)
                pool.wait_ge(pool_chain, links[0])

            pool.memset(w02[:], 0.0).then_inc(zeroed, 1)
            pool.memset(w1oh[:], 0.0).then_inc(zeroed, 1)
            pool.memset(w1ho[:], 0.0).then_inc(zeroed, 1)
            pool.memset(vS[:, :, :, D:D + VPAD], 0.0).then_inc(consts, 1)
            link(pool.memset(halfc[:, 0:8], -0.5))
            link(pool.memset(halfc[:, 8:16], 0.5))
            pool.wait_ge(l_par, 16)
            pool.wait_ge(l_small, 16)
            link(pool.tensor_scalar(qknw[:, 0:D], qknw[:, 0:D], HD ** -0.5, None, ALU.mult))
            link(pool.tensor_scalar(scl, scl, 0.5, None, ALU.mult))
            link(pool.tensor_scalar(lrb, lrb, BASE_LR_INV, None, ALU.add))
            nw = qknw.rearrange("p (h k d) -> p h k d", k=2, d=8)
            for t in range(2):
                co = cosw[:, t].rearrange("p (h k d) -> p h k d", k=2, d=8)
                si_ = sinw[:, t].rearrange("p (h k d) -> p h k d", k=2, d=8)
                for k in range(2):
                    def angle(a):
                        return trig[:, t, a].unsqueeze(1).broadcast_to([P, 2 * H, 8])
                    pool.tensor_tensor(co[:, :, k], nw[:, :, k], angle(0), ALU.mult)
                    last = pool.tensor_tensor(si_[:, :, k], nw[:, :, 1 - k], angle(1 + k), ALU.mult)
            last.then_inc(trig_ready, 1)

            for step in SCHEDULE:
                kind, n = step[0], step[1] if len(step) > 1 else 0
                if kind == "L":
                    s = n % 2
                    pool.wait_ge(ln_stats, n + 1)
                    link(pool.tensor_scalar(lve[:, s:s + 1], lmv[:, s, 1:2], 1e-5, None, ALU.add))
                    pool.tensor_tensor(lrs[:, s:s + 1], lve[:, s:s + 1], halfc[:, 0:1], ALU.pow).then_inc(ln_rstd, 1)
                elif kind == "G":
                    pool.wait_ge(fstats, n + 1)
                    link(pool.tensor_scalar(fve[:], fmv[:, :, 1], 1e-5, None, ALU.add))
                    pool.tensor_tensor(frs[:], fve[:], halfc[:, 0:2], ALU.pow).then_inc(frstd, 1)
                elif kind == "F":
                    i = step[2]
                    m = n * FT + i
                    pool.wait_ge(gated, m + 1)
                    if m >= 3:
                        pool.wait_ge(down_done, m - 2)
                    if m == 0:
                        pool.wait_ge(coefx_ready, FT // 2)
                    pool.tensor_tensor(fh[:, m % 3], fb[:, m % 2], coefx[:, i], ALU.mult).then_inc(h_ready, 1)
                elif kind == "P2":
                    s, t = n % 2, ORDER[n][1]
                    pool.wait_ge(ss_ready, n + 1)
                    link(pool.tensor_scalar(msqk[:, s], ssqk[:, s], 1.0 / D, 1e-6, ALU.mult, ALU.add))
                    pool.tensor_tensor(rqk[:, s], msqk[:, s], halfc[:, 0:2], ALU.pow).then_inc(rqk_ready, 1)
                    pool.wait_ge(silu_ready, n + 1)
                    if n >= 1:
                        pool.wait_ge(fn_ready, n)
                        pool.wait_ge(rope_ready, n)
                    link(pool.tensor_tensor(f1[:], s2[:], scl, ALU.mult))
                    pool.tensor_tensor(f2[:], f1[:], off, ALU.add).then_inc(f_ready, 1)
                    pool.wait_ge(qk_scaled, n + 1)
                    pool.wait_ge(f_ready, n + 1)
                    if n == 0:
                        pool.wait_ge(trig_ready, 1)
                    pool.tensor_tensor(rp1[:], qks[:], cosw[:, t], ALU.mult)
                    src = qks[:].rearrange("p (h k d) -> p h k d", k=2, d=8)
                    dst = rp2.rearrange("p (h k d) -> p h k d", k=2, d=8)
                    tab = sinw[:, t].rearrange("p (h k d) -> p h k d", k=2, d=8)
                    pool.tensor_tensor(dst[:, :, 0], src[:, :, 1], tab[:, :, 0], ALU.mult)
                    link(pool.tensor_tensor(dst[:, :, 1], src[:, :, 0], tab[:, :, 1], ALU.mult))
                    pool.tensor_tensor(rope[:], rp1[:], rp2, ALU.add).then_inc(rope_ready, 1)
                elif kind == "N":
                    s = n % 2
                    pool.wait_ge(ss8_ready, n + 1)
                    pool.tensor_tensor(nrm[:], ss8[:], halfc[:, 8:16], ALU.pow).then_inc(nrm_ready, 1)
                    pool.wait_ge(rz_ready, n + 1)
                    link(pool.tensor_tensor(lz[:, 0], ez[:], rz[:], ALU.mult))
                    link(pool.tensor_tensor(lz[:, 1], lz[:, 0], lz[:, 0], ALU.mult))
                    link(pool.tensor_scalar(lz[:, 2], lz[:, 1], 1 / 17, 1 / 15, ALU.mult, ALU.add))
                    for j, c in enumerate([13, 11, 9, 7, 5, 3, 1]):
                        link(pool.tensor_tensor(lz[:, 3 + 2 * j], lz[:, 2 + 2 * j], lz[:, 1], ALU.mult))
                        link(pool.tensor_scalar(lz[:, 4 + 2 * j], lz[:, 3 + 2 * j], 1 / c, None, ALU.add))
                    link(pool.tensor_tensor(lz[:, 17], lz[:, 16], lz[:, 0], ALU.mult))
                    link(pool.tensor_scalar(lz[:, 18], lz[:, 17], 2.0, None, ALU.mult))
                    link(pool.tensor_tensor(lr[:, s], lz[:, 18], z[:, 2], ALU.add))
                    pool.tensor_scalar(lrh[:, s], lr[:, s, NH:2 * NH], 0.5, None, ALU.mult).then_inc(lr_ready, 1)
                elif kind == "Ta":
                    s = n % 2
                    pool.wait_ge(grads_ready, n + 1)
                    pool.wait_ge(lr_ready, n + 1)
                    if n >= 1:
                        pool.wait_ge(tb_psum, n)
                    for p in range(NPAIR):
                        cols, hs = slice(p * P, (p + 1) * P), slice(2 * p, 2 * p + 2)
                        pool.tensor_tensor(heads(dd[:, p, 0], 2, FD), heads(dg[:, cols], 2, FD),
                                           spread(lr[:, s, 0:NH][:, hs], 2, FD), ALU.mult)
                        pool.tensor_tensor(heads(dd[:, p, 1], 2, FD), heads(dhp[:, cols], 2, FD),
                                           spread(lr[:, s, 2 * NH:3 * NH][:, hs], 2, FD), ALU.mult)
                    pool.tensor_tensor(heads(vl[:], NH, FD), heads(s2v[:, s], NH, FD),
                                       spread(lrh[:, s], NH, FD), ALU.mult).then_inc(dd_ready, 1)
                elif kind == "Tc2":
                    pool.wait_ge(ss4_ready, n + 1)
                    link(pool.tensor_scalar(ms4[:], ss4[:], 1.0 / FD, 1e-6, ALU.mult, ALU.add))
                    pool.tensor_tensor(r4[:], ms4[:], halfc[:, 0:NH], ALU.pow).then_inc(r4_ready, 1)
                elif kind == "Tc3":
                    pool.wait_ge(tt_ready, n + 1)
                    pool.tensor_tensor(heads(ttw[:], NH, FD), heads(tt[:], NH, FD),
                                       ttw_w.unsqueeze(1).broadcast_to([P, NH, FD]), ALU.mult).then_inc(ttw_ready, 1)
                elif kind == "O1":
                    pool.wait_ge(attn_ready, n + 1)
                    pool.wait_ge(ttw_ready, n + 1)
                    pool.tensor_tensor(yS[:], aS[:], ttw[:], ALU.add).then_inc(y_ready, 1)

        @block.scalar
        def _(act):
            links = [0]

            def link(ins):
                links[0] += 1
                ins.then_inc(act_chain, 1)
                act.wait_ge(act_chain, links[0])

            for step in SCHEDULE:
                kind, n = step[0], step[1] if len(step) > 1 else 0
                if kind == "C":
                    for i in range(0, FT // 2, 2):
                        act.wait_ge(coefx_psum, i + 1)
                        act.activation(coefx[:, 2 * i:2 * i + 2], heads(GU[i % 2][:], 2, D), ACT.Copy)\
                           .then_inc(coefx_ready, 1)
                        if i + 1 < FT // 2:
                            act.wait_ge(coefx_psum, i + 2)
                            act.activation(coefx[:, 2 * i + 2:2 * i + 4], heads(GU[1][:], 2, D), ACT.Copy)\
                               .then_inc(coefx_ready, 1)
                elif kind == "G1":
                    act.wait_ge(fxT_psum, n + 1)
                    act.activation(fxT[:], heads(GU[0][:], DK, 2 * P), ACT.Copy).then_inc(fxT_ready, 1)
                elif kind == "F":
                    m = n * FT + step[2]
                    act.wait_ge(gu_ready, m + 1)
                    if m >= 2:
                        act.wait_ge(gated, m - 1)
                    act.activation(fth[:, m % 2], GU[m % 2][:, 0:D], ACT.Tanh, scale=0.5).then_inc(fth_ready, 1)
                elif kind == "P1":
                    act.wait_ge(xnT_psum, n + 1)
                    if n >= 1:
                        act.wait_ge(qkv_ready, n)
                    act.activation(xnT[:], heads(X[:, 0:D], DK, P), ACT.Copy).then_inc(xnT_ready, 1)
                elif kind == "P2":
                    (b, t), s = ORDER[n], n % 2
                    act.wait_ge(qkv_ready, n + 1)
                    if n >= 1:
                        act.wait_ge(qkT_psum, n)
                    act.activation(qks[:], X[:], ACT.Copy)
                    act.activation(vS[:, KV_SLOT[b], t, 0:D], Y[:, 0:D], ACT.Copy)
                    if n >= 1:
                        act.wait_ge(lr_ready, n)
                    act.activation(z[:, 4], Y[:, D:D + 3 * NH], ACT.Copy).then_inc(qkv_sb, 1)
                    act.wait_ge(qkv_sb, n + 1)
                    link(act.activation(sqs[:, 0:D], qks[:, 0:D], ACT.Square, accum_out=ssqk[:, s, 0:1]))
                    act.activation(sqs[:, D:2 * D], qks[:, D:2 * D], ACT.Square, accum_out=ssqk[:, s, 1:2])\
                       .then_inc(ss_ready, 1)
                    if n >= 1:
                        act.wait_ge(rope_ready, n)
                    act.activation(th[:, 0:512], qks[:], ACT.Tanh, scale=0.5)
                    act.activation(th[:, 512:768], vS[:, KV_SLOT[b], t, 0:D], ACT.Tanh, scale=0.5).then_inc(th_ready, 1)
                    act.wait_ge(silu_ready, n + 1)
                    act.activation(ez[:], z[:, 1], ACT.Exp, scale=-1.0).then_inc(ez_ready, 1)
                elif kind == "N":
                    act.wait_ge(f_ready, n + 1)
                    act.activation(sqf[:], f2[:], ACT.Square).then_inc(sqf_ready, 1)
                elif kind == "P3":
                    act.wait_ge(fT_psum, n + 1)
                    if n >= 1:
                        act.wait_ge(gq_psum, n)
                    act.activation(fT[:], heads(X[:], 4, P), ACT.Copy).then_inc(fT_ready, 1)
                elif kind == "P4":
                    act.wait_ge(fvT_psum, n + 1)
                    if n >= 1:
                        act.wait_ge(ta_psum, n)
                    act.activation(fvT[:], heads(X[:, 0:D], NPAIR, P), ACT.Copy, scale=0.5).then_inc(fvT_ready, 1)
                elif kind == "S":
                    u, t, s = step[2], ORDER[n][1], n % 2
                    q = UBASE[n] + u
                    nh = 4 if t == 0 else 2
                    w = 512 // nh
                    act.wait_ge(nmax_ready, q + 1)
                    if q >= 2:
                        act.wait_ge(pT_psum, q - 1)
                    for a, h in enumerate(unit_heads(t, u)):
                        ins = act.activation(pS[:, q % 2, a * w:(a + 1) * w], SC[:, a * w:(a + 1) * w], ACT.Exp,
                                             bias=nmax[:, q % 2, a:a + 1], accum_out=rsum[:, s, h:h + 1])
                    ins.then_inc(exp_done, 1)
                elif kind == "T":
                    q = UBASE[n] + step[2]
                    if q % 2:
                        act.wait_ge(pT_psum, q + 1)
                        act.wait_ge(pv_done, q - 1)
                        act.activation(pT[:, q % 2], PT[:], ACT.Copy).then_inc(pT_ready, 1)
                elif kind == "Ta":
                    act.wait_ge(ta_psum, n + 1)
                    gate = X[:].rearrange("p (h k d) -> p h k d", h=NPAIR, k=2)[:, :, 0]
                    act.activation(heads(ta[:], NPAIR, P), gate, ACT.Tanh, scale=0.5).then_inc(ta_ready, 1)
                elif kind == "Tc1":
                    act.wait_ge(gq_psum, n + 1)
                    gate = X[:].rearrange("p (h k c) -> p h k c", h=NPAIR, k=2)[:, :, 0]
                    act.activation(heads(tq[:], NPAIR, P), gate, ACT.Tanh, scale=0.5).then_inc(tq_ready, 1)
                elif kind == "Tc2":
                    act.wait_ge(oi_psum, n + 1)
                    act.activation(sqo[:], Y[:, 0:D], ACT.Square).then_inc(sqo_ready, 1)
                elif kind == "O2":
                    act.wait_ge(yT_psum, n + 1)
                    act.activation(yT[:], heads(Y[:, 0:D], DK, P), ACT.Copy).then_inc(yT_ready, 1)

        @block.vector
        def _(dve):
            links = [0]

            def link(ins):
                links[0] += 1
                ins.then_inc(dve_chain, 1)
                dve.wait_ge(dve_chain, links[0])

            dve.wait_ge(l_ident, 16)
            dve.tensor_copy(identb[:], ident[:])
            dve.wait_ge(l_mask, 16)
            dve.tensor_copy(mask[:], maskf[:]).then_inc(masks_ready, 1)

            for step in SCHEDULE:
                kind, n = step[0], step[1] if len(step) > 1 else 0
                if kind == "C":
                    dve.wait_ge(l_route, 32)
                    dve.wait_ge(l_small, 16)
                    link(dve.tensor_copy(idx_f[:], idx_i[:]))
                    for t in range(2):
                        for k in range(TOPK):
                            last = dve.tensor_scalar(coef1[:, t, k], expert_no, idx_f[:, t, k:k + 1],
                                                     topw[:, t, k:k + 1], ALU.is_equal, ALU.mult)
                    link(last)
                    link(dve.tensor_reduce(coef[:], coef1[:].rearrange("p t k e -> p t e k"), AX.X, ALU.add))
                    link(dve.tensor_copy(coef3[:, :, 0:E], coef[:]))
                    link(dve.tensor_tensor(coef_r[:, 0], coef[:], coef3[:, :, 0:E], ALU.subtract))
                    link(dve.tensor_copy(coef3[:, :, E:2 * E], coef_r[:, 0]))
                    link(dve.tensor_tensor(coef_r[:, 1], coef_r[:, 0], coef3[:, :, E:2 * E], ALU.subtract))
                    dve.tensor_copy(coef3[:, :, 2 * E:3 * E], coef_r[:, 1]).then_inc(coef_ready, 1)
                    dve.wait_ge(coefT_psum, 1)
                    dve.tensor_copy(coefT[:], GU[1][:].bitcast(BF16)[0:3 * E, 0:2 * P]).then_inc(coefT_ready, 1)
                elif kind == "L":
                    (b, t), s = ORDER[n], n % 2
                    dve.wait_ge(l_x[b], 16)
                    if b == 0:
                        dve.wait_ge(ffn_added, 1)
                    link(dve.bn_stats(lst[:, s], xs[:, b, t]))
                    dve.bn_aggr(lmv[:, s], lst[:, s]).then_inc(ln_stats, 1)
                elif kind == "G":
                    dve.wait_ge(l_x[0], 16)
                    if n == 1:
                        dve.wait_ge(x2_ready, ORDER.index((0, 1)) + 1)
                    dve.bn_stats(fst[:, 0], xs[:, 0, 0])
                    link(dve.bn_stats(fst[:, 1], xs[:, 0, 1]))
                    dve.bn_aggr(fmv[:, 0], fst[:, 0])
                    dve.bn_aggr(fmv[:, 1], fst[:, 1]).then_inc(fstats, 1)
                elif kind == "G1":
                    dve.wait_ge(frstd, n + 1)
                    for t in range(2):
                        last = dve.tensor_scalar(fxn[:, t], xs[:, 0, t], fmv[:, t, 0:1], frs[:, t:t + 1],
                                                 ALU.subtract, ALU.mult)
                    last.then_inc(fxn_ready, 1)
                elif kind == "F":
                    m = n * FT + step[2]
                    s, G = m % 2, GU[m % 2]
                    dve.wait_ge(fth_ready, m + 1)
                    if m >= 1:
                        dve.wait_ge(gated, m)
                    if m >= 2:
                        dve.wait_ge(h_ready, m - 1)
                    link(dve.scalar_tensor_tensor(fa[:], fth[:, s], 1.0, G[:, 0:D], ALU.add, ALU.mult))
                    dve.tensor_tensor(fb[:, s], fa[:], G[:, D:2 * D], ALU.mult).then_inc(gated, 1)
                elif kind == "FE":
                    dve.wait_ge(down_done, (n + 1) * FT)
                    x0 = xs[:, 0].rearrange("p t d -> p (t d)")
                    dve.tensor_tensor(x0, x0, DN[:], ALU.add).then_inc(ffn_added, 1)
                elif kind == "P1":
                    (b, t), s = ORDER[n], n % 2
                    dve.wait_ge(ln_rstd, n + 1)
                    if n >= 1:
                        dve.wait_ge(xnT_psum, n)
                    dve.tensor_scalar(xn[:], xs[:, b, t], lmv[:, s, 0:1], lrs[:, s:s + 1],
                                      ALU.subtract, ALU.mult).then_inc(xn_ready, 1)
                elif kind == "P2":
                    (b, t), s = ORDER[n], n % 2
                    dve.wait_ge(trig_ready, 1)
                    dve.wait_ge(th_ready, n + 1)
                    if n >= 1:
                        dve.wait_ge(f_ready, n)
                    dve.scalar_tensor_tensor(s2[:], th[:, 0:512], 1.0, qks[:], ALU.add, ALU.mult)
                    dve.scalar_tensor_tensor(s2v[:, s], th[:, 512:768], 1.0, vS[:, KV_SLOT[b], t, 0:D],
                                             ALU.add, ALU.mult)
                    link(dve.tensor_tensor(z[:, 0], z[:, 4], lrb, ALU.add))
                    dve.tensor_scalar(z[:, 2], z[:, 0], 0.0, None, ALU.max)
                    link(dve.tensor_scalar(z[:, 3], z[:, 0], -1.0, None, ALU.mult))
                    dve.tensor_tensor(z[:, 1], z[:, 0], z[:, 3], ALU.max).then_inc(silu_ready, 1)
                    dve.wait_ge(rqk_ready, n + 1)
                    dve.wait_ge(silu_ready, n + 1)
                    dve.tensor_scalar(qks[:, 0:D], qks[:, 0:D], rqk[:, s, 0:1], None, ALU.mult)
                    dve.tensor_scalar(qks[:, D:2 * D], qks[:, D:2 * D], rqk[:, s, 1:2], None, ALU.mult)\
                       .then_inc(qk_scaled, 1)
                elif kind == "N":
                    dve.wait_ge(sqf_ready, n + 1)
                    dve.tensor_reduce(ss8[:], heads(sqf[:], 2 * NH, FD), AX.X, ALU.add).then_inc(ss8_ready, 1)
                    dve.wait_ge(ez_ready, n + 1)
                    link(dve.tensor_scalar(z[:, 3], ez[:], 2.0, None, ALU.add))
                    dve.reciprocal(rz[:], z[:, 3]).then_inc(rz_ready, 1)
                elif kind == "N2":
                    s = n % 2
                    dve.wait_ge(nrm_ready, n + 1)
                    link(dve.tensor_scalar(inv8[:, 0], nrm[:], 1e-12, None, ALU.add))
                    link(dve.reciprocal(inv8[:, 1], inv8[:, 0]))
                    if n >= 1:
                        dve.wait_ge(tb_psum, n)
                    dve.tensor_tensor(heads(fn[:], 2 * NH, FD), heads(f2[:], 2 * NH, FD),
                                      spread(inv8[:, 1], 2 * NH, FD), ALU.mult).then_inc(fn_ready, 1)
                elif kind == "P3":
                    (b, t), s = ORDER[n], n % 2
                    dve.wait_ge(qkT_psum, n + 1)
                    dve.tensor_copy(kT[:, KV_SLOT[b], :, t * P:(t + 1) * P], heads(Y[:, D:2 * D], 2, P))
                    for k in range(2):
                        last = dve.tensor_scalar(qTm[:, s, k], heads(Y[:, 0:D], 2, P), head_mask[:, k:k + 1], None,
                                                 ALU.mult)
                    last.then_inc(qkT_ready, 1)
                elif kind == "S":
                    nh = 4 if ORDER[n][1] == 0 else 2
                    q = UBASE[n] + step[2]
                    dve.wait_ge(scores_ready, q + 1)
                    dve.tensor_reduce(nmax[:, q % 2, 0:nh], heads(SC[:], nh, 512 // nh), AX.X, ALU.max, negate=True)\
                       .then_inc(nmax_ready, 1)
                elif kind == "T":
                    q = UBASE[n] + step[2]
                    if q % 2 == 0:
                        dve.wait_ge(pT_psum, q + 1)
                        if q >= 2:
                            dve.wait_ge(pv_done, q - 1)
                        dve.tensor_copy(pT[:, q % 2], PT[:]).then_inc(pT_ready, 1)
                elif kind == "O0":
                    dve.wait_ge(pv_done, UBASE[n + 1])
                    if n >= 1:
                        dve.wait_ge(attn_ready, n)
                    dve.reciprocal(rinv[:], rsum[:, n % 2])
                    dve.tensor_copy(oS[:], OT[:]).then_inc(oS_ready, 1)
                elif kind == "O1":
                    dve.wait_ge(o_psum, n + 1)
                    dve.wait_ge(oS_ready, n + 1)
                    if n >= 1:
                        dve.wait_ge(y_ready, n)
                    o = X[:].rearrange("p (h w) -> p h w", w=2 * HD)[:, :, 0:HD]
                    dve.tensor_tensor(heads(aS[:], H, HD), o, spread(rinv[:], H, HD), ALU.mult)\
                       .then_inc(attn_ready, 1)
                elif kind == "O3":
                    b, t = ORDER[n]
                    dve.wait_ge(wo_psum, n + 1)
                    dve.tensor_tensor(xs[:, b, t], xs[:, b, t], X[:, 0:D], ALU.add).then_inc(x2_ready, 1)
                elif kind == "Ta":
                    g = X[:].rearrange("p (h k d) -> p h k d", h=NPAIR, k=2)
                    gate, up, dh = g[:, :, 0], g[:, :, 1], heads(Y[:, 0:D], NPAIR, P)
                    dve.wait_ge(ta_ready, n + 1)
                    if n >= 1:
                        dve.wait_ge(dd_ready, n)
                        dve.wait_ge(tb_psum, n)
                    link(dve.tensor_scalar(sg[:], ta[:], 0.5, 0.5, ALU.mult, ALU.add))
                    link(dve.tensor_tensor(heads(si[:], NPAIR, P), heads(sg[:], NPAIR, P), gate, ALU.mult))
                    dve.tensor_tensor(heads(hid[:], NPAIR, P), heads(si[:], NPAIR, P), up, ALU.mult)
                    dve.tensor_tensor(heads(dhp[:], NPAIR, P), heads(si[:], NPAIR, P), dh, ALU.mult)
                    link(dve.tensor_tensor(heads(q1[:], NPAIR, P), gate, heads(si[:], NPAIR, P), ALU.subtract))
                    link(dve.scalar_tensor_tensor(q3[:], q1[:], 1.0, sg[:], ALU.add, ALU.mult))
                    link(dve.tensor_tensor(heads(tg[:], NPAIR, P), heads(q3[:], NPAIR, P), dh, ALU.mult))
                    dve.tensor_tensor(heads(dg[:], NPAIR, P), heads(tg[:], NPAIR, P), up, ALU.mult).then_inc(grads_ready, 1)
                elif kind == "Tb":
                    old, new, t = w_old(n), KV_SLOT[ORDER[n][0]], ORDER[n][1]
                    dve.wait_ge(tb_psum, n + 1)
                    dve.wait_ge(l_init, 16 * 3 * NH)
                    dve.wait_ge(zeroed, 3)
                    for a in range(2):
                        rows = slice(FD * a, FD * a + FD)
                        c1 = slice(FD * a, FD * (a + 1))
                        dve.tensor_tensor(w02[rows, new, :, :, c1], w02[rows, old, :, :, c1],
                                          X[rows, :].rearrange("p (n k c) -> p n k c", n=NPAIR, k=2)[:, :, :, c1],
                                          ALU.add)
                        if t == 0:
                            dve.tensor_tensor(w1oh[rows, new, :, c1], w1oh[rows, old, :, c1],
                                              heads(Y[rows, D:2 * D], NPAIR, 2 * FD)[:, :, c1], ALU.add)
                        last = dve.tensor_tensor(w1ho[rows, new, :, c1], w1ho[rows, old, :, c1],
                                                 heads(Y[rows, 0:D], NPAIR, 2 * FD)[:, :, c1], ALU.add)
                    last.then_inc(w_updated, 1)
                elif kind == "Tc1":
                    g = X[:].rearrange("p (h k c) -> p h k c", h=NPAIR, k=2)
                    dve.wait_ge(tq_ready, n + 1)
                    if n >= 1:
                        dve.wait_ge(oi_psum, n)
                    link(dve.scalar_tensor_tensor(heads(sq2[:], NPAIR, P), heads(tq[:], NPAIR, P), 1.0, g[:, :, 0],
                                                  ALU.add, ALU.mult))
                    dve.scalar_tensor_tensor(hqT[:], heads(sq2[:], NPAIR, P), 0.5, g[:, :, 1], ALU.mult, ALU.mult)\
                       .then_inc(hq_ready, 1)
                elif kind == "Tc2":
                    dve.wait_ge(sqo_ready, n + 1)
                    dve.tensor_reduce(ss4[:], heads(sqo[:], NH, FD), AX.X, ALU.add).then_inc(ss4_ready, 1)
                elif kind == "Tc3":
                    dve.wait_ge(r4_ready, n + 1)
                    if n >= 1:
                        dve.wait_ge(yT_psum, n)
                    dve.tensor_tensor(heads(tt[:], NH, FD), heads(Y[:, 0:D], NH, FD), spread(r4[:], NH, FD), ALU.mult)\
                       .then_inc(tt_ready, 1)

        @block.tensor
        def _(pe):
            def wait_all(*pairs):
                for s, v in pairs:
                    pe.wait_ge(s, v)

            pe.wait_ge(l_ident, 16)
            for step in SCHEDULE:
                kind, n = step[0], step[1] if len(step) > 1 else 0
                if kind == "C":
                    pe.wait_ge(coef_ready, 1)
                    for t in range(2):
                        mm = pe.transpose(GU[1][:].bitcast(BF16)[0:3 * E, t * P:(t + 1) * P], coef3[:, t], identb[:])
                    mm.then_inc(coefT_psum, 1)
                    pe.wait_ge(coefT_ready, 1)
                    pe.wait_ge(l_expand, 16)
                    pe.wait_ge(fxT_ready, 1)
                    for i in range(FT):
                        j = i // 2
                        if i % 2 == 0 and j >= 2:
                            pe.wait_ge(coefx_ready, j - 1)
                        mm = pe.matmul(GU[j % 2][:, (i % 2) * D:(i % 2 + 1) * D], expand[:, i * P:(i + 1) * P],
                                       coefT[:], start=True, stop=True)
                        if i % 2:
                            mm.then_inc(coefx_psum, 1)
                elif kind == "G1":
                    pe.wait_ge(fxn_ready, n + 1)
                    if n:
                        pe.wait_ge(gated, n * FT)
                    for t in range(2):
                        for k in range(DK):
                            mm = pe.transpose(GU[0][:, k * D + t * P:k * D + (t + 1) * P], fxn[:, t, k * P:(k + 1) * P],
                                              ident[:])
                    mm.then_inc(fxT_psum, 1)
                elif kind == "F":
                    i = step[2]
                    m = n * FT + i
                    if i == 0:
                        pe.wait_ge(fxT_ready, n + 1)
                        if n == 0:
                            pe.wait_ge(coefx_ready, FT // 2)
                    if n == 0:
                        pe.wait_ge(l_wff[i // 2], 16)
                    if m >= 2:
                        pe.wait_ge(gated, m - 1)
                    for g in range(2):
                        for k in range(DK):
                            mm = pe.matmul(GU[m % 2][:, g * D:(g + 1) * D], wff[:, i, (2 * g + k) * P:(2 * g + k + 1) * P],
                                           fxT[:, k], start=(k == 0), stop=(k == DK - 1))
                    mm.then_inc(gu_ready, 1)
                elif kind == "D":
                    i = step[2]
                    m = n * FT + i
                    pe.wait_ge(h_ready, m + 1)
                    if i == 0 and n:
                        pe.wait_ge(ffn_added, n)
                    for t in range(2):
                        mm = pe.matmul(DN[:, t * D:(t + 1) * D], fh[:, m % 3, t * P:(t + 1) * P],
                                       wff[:, i, 2 * D:3 * D], start=(i == 0 and t == 0), stop=(i == FT - 1),
                                       skip_group_check=True)
                    mm.then_inc(down_done, 1)
                elif kind == "P1":
                    pe.wait_ge(xn_ready, n + 1)
                    if n >= 2:
                        pe.wait_ge(attn_ready, n - 1)
                    elif n == 1:
                        pe.wait_ge(fvT_ready, 1)
                    for k in range(DK):
                        mm = pe.transpose(X[:, k * P:(k + 1) * P], xn[:, k * P:(k + 1) * P], ident[:])
                    mm.then_inc(xnT_psum, 1)
                elif kind == "P2":
                    s = n % 2
                    pe.wait_ge(xnT_ready, n + 1)
                    if n == 0:
                        pe.wait_ge(l_wqkv, 16)
                    else:
                        pe.wait_ge(grads_ready, n)
                    if n >= 2:
                        pe.wait_ge(yT_ready, n - 1)
                    for k in range(DK):
                        pe.matmul(X[:], xnT[:, k], wqkv[:, k, 0:512], start=(k == 0), stop=(k == DK - 1))
                    for k in range(DK):
                        mm = pe.matmul(Y[:, 0:D + 3 * NH], xnT[:, k], wqkv[:, k, 512:], start=(k == 0),
                                       stop=(k == DK - 1))
                    mm.then_inc(qkv_ready, 1)
                elif kind == "P3":
                    s = n % 2
                    pe.wait_ge(fn_ready, n + 1)
                    if n == 0:
                        pe.wait_ge(qkv_sb, 1)
                    else:
                        wait_all((hq_ready, n), (w_updated, n))
                    for j in range(4):
                        mm = pe.transpose(X[:, j * P:(j + 1) * P], fn[:, j * P:(j + 1) * P], ident[:])
                    mm.then_inc(fT_psum, 1)
                    pe.wait_ge(rope_ready, n + 1)
                    for j in range(4):
                        mm = pe.transpose(Y[:, j * P:(j + 1) * P], rope[:, j * P:(j + 1) * P], ident[:])
                    mm.then_inc(qkT_psum, 1)
                elif kind == "P4":
                    pe.wait_ge(fT_ready, n + 1)
                    for j in range(NPAIR):
                        mm = pe.transpose(X[:, j * P:(j + 1) * P], s2v[:, n % 2, j * P:(j + 1) * P],
                                          ident[:])
                    mm.then_inc(fvT_psum, 1)
                elif kind == "S":
                    (b, t), u, s = ORDER[n], step[2], n % 2
                    q = UBASE[n] + u
                    nh = 4 if t == 0 else 2
                    w = 512 // nh
                    if u == 0:
                        pe.wait_ge(qkT_ready, n + 1)
                        pe.wait_ge(masks_ready, 1)
                    if q:
                        pe.wait_ge(exp_done, q)
                    added = mask[:, t * P:t * P + w].unsqueeze(1).broadcast_to([P, nh, w])
                    pe.matmul(SC[:], identb[:], added, start=True, stop=False, skip_group_check=True)
                    for a, h in enumerate(unit_heads(t, u)):
                        c, j, par_ = h // 8, (h % 8) // 2, h % 2
                        rows = slice(32 * j, 32 * j + 32)
                        mm = pe.matmul(SC[:, a * w:(a + 1) * w], qTm[rows, s, par_, c], kT[rows, KV_SLOT[b], c, 0:w],
                                       start=False, stop=(a == nh - 1), skip_group_check=True)
                    mm.then_inc(scores_ready, 1)
                elif kind == "T":
                    q = UBASE[n] + step[2]
                    pe.wait_ge(exp_done, q + 1)
                    if q:
                        pe.wait_ge(pT_ready, q)
                    for j in range(4):
                        mm = pe.transpose(PT[:, j * P:(j + 1) * P], pS[:, q % 2, j * P:(j + 1) * P], ident[:])
                    mm.then_inc(pT_psum, 1)
                elif kind == "V":
                    (b, t), u = ORDER[n], step[2]
                    q = UBASE[n] + u
                    pe.wait_ge(pT_ready, q + 1)
                    if u == 0:
                        pe.wait_ge(qkv_sb, n + 1)
                        pe.wait_ge(consts, 1)
                        if n:
                            pe.wait_ge(oS_ready, n)
                    for a, h in enumerate(unit_heads(t, u)):
                        g, j = h // 4, h % 4
                        for k in range(t + 1):
                            mm = pe.matmul(OT[32 * j:32 * j + 32, g * P:(g + 1) * P], vS[:, KV_SLOT[b], k, HD * h:HD * h + 32],
                                           pT[:, q % 2, (a * (t + 1) + k) * P:(a * (t + 1) + k + 1) * P],
                                           start=(k == 0), stop=(k == t))
                    mm.then_inc(pv_done, 1)
                elif kind == "O1":
                    pe.wait_ge(oS_ready, n + 1)
                    if n + 1 < NT:
                        pe.wait_ge(fvT_ready, n + 2)
                    else:
                        pe.wait_ge(hq_ready, n + 1)
                    for j in range(4):
                        mm = pe.transpose(X[:, j * P:(j + 1) * P], oS[:, j * P:(j + 1) * P], ident[:])
                    mm.then_inc(o_psum, 1)
                elif kind == "O2":
                    pe.wait_ge(y_ready, n + 1)
                    if n + 1 < NT:
                        pe.wait_ge(grads_ready, n + 2)
                    else:
                        pe.wait_ge(tt_ready, n + 1)
                    for k in range(DK):
                        mm = pe.transpose(Y[:, k * P:(k + 1) * P], yS[:, k * P:(k + 1) * P], ident[:])
                    mm.then_inc(yT_psum, 1)
                elif kind == "O3":
                    pe.wait_ge(yT_ready, n + 1)
                    if n + 2 < NT:
                        pe.wait_ge(qkv_sb, n + 3)
                    elif n + 1 < NT:
                        pe.wait_ge(grads_ready, n + 2)
                    else:
                        pe.wait_ge(attn_ready, n + 1)
                    if n == 0:
                        pe.wait_ge(l_wo, 16)
                    for k in range(DK):
                        mm = pe.matmul(X[:, 0:D], yT[:, k], wo[:, k], start=(k == 0), stop=(k == DK - 1))
                    mm.then_inc(wo_psum, 1)
                elif kind == "Ta":
                    s, old = n % 2, w_old(n)
                    wait_all((fT_ready, n + 1), (fvT_ready, n + 1))
                    if old == INIT:
                        wait_all((l_init, 16 * 3 * NH), (zeroed, 3))
                    else:
                        pe.wait_ge(w_updated, ORDER.index((ORDER[n][0], 0)) + 1)
                    if n + 1 < NT:
                        pe.wait_ge(xnT_ready, n + 2)
                    else:
                        pe.wait_ge(attn_ready, n)
                    if n:
                        pe.wait_ge(tt_ready, n)
                    else:
                        pe.wait_ge(qkT_ready, 1)
                    for p in range(NPAIR):
                        pe.matmul(X[:, p * D:(p + 1) * D], fT[:, 2 + p], w02[:, old, p], start=True, stop=True)
                    for p in range(NPAIR):
                        mm = pe.matmul(Y[:, p * P:(p + 1) * P], fvT[:, p], w1oh[:, old, p], start=True, stop=True)
                    mm.then_inc(ta_psum, 1)
                elif kind == "Tb":
                    s, t = n % 2, ORDER[n][1]
                    pe.wait_ge(dd_ready, n + 1)
                    if n:
                        pe.wait_ge(x2_ready, n)
                    if n + 1 < NT:
                        pe.wait_ge(qkv_sb, n + 2)
                    else:
                        pe.wait_ge(yT_ready, n)
                    for p in range(NPAIR):
                        cols = slice(p * P, (p + 1) * P)
                        kcols = slice(D + p * P, D + (p + 1) * P)
                        pe.matmul(X[:, p * D:(p + 1) * D], fn[:, kcols], dd[:, p], start=True, stop=True)
                        mm = pe.matmul(Y[:, cols], hid[:, cols], vl[:, cols], start=True, stop=True)
                        if t == 0:
                            mm = pe.matmul(Y[:, kcols], vl[:, cols], hid[:, cols], start=True, stop=True)
                    mm.then_inc(tb_psum, 1)
                elif kind == "Tc1":
                    new = KV_SLOT[ORDER[n][0]]
                    pe.wait_ge(w_updated, n + 1)
                    for p in range(NPAIR):
                        for k in range(2):
                            mm = pe.matmul(X[:, p * D + k * P:p * D + (k + 1) * P], w02[:, new, p, k], fT[:, p],
                                           start=True, stop=True)
                    mm.then_inc(gq_psum, 1)
                elif kind == "Tc2":
                    pe.wait_ge(hq_ready, n + 1)
                    if n + 1 < NT:
                        pe.wait_ge(qkT_ready, n + 2)
                    for p in range(NPAIR):
                        mm = pe.matmul(Y[:, p * P:(p + 1) * P], hqT[:, p], w1ho[:, KV_SLOT[ORDER[n][0]], p], start=True, stop=True)
                    mm.then_inc(oi_psum, 1)


def kernel(**inputs):
    import numpy as np
    import concourse.bacc as bacc
    from concourse.bass_utils import run_bass_kernel_spmd

    def get(name):
        return np.asarray(inputs[name])

    f32 = np.float32
    gate = get("L0_ffn_gate_weight").reshape(E * I, D).T.reshape(DK, P, FT, P)
    up = get("L0_ffn_up_weight").reshape(E * I, D).T.reshape(DK, P, FT, P)
    down = get("L0_ffn_down_weight").transpose(0, 2, 1).reshape(FT, P, D)
    wff = np.concatenate([gate[0], gate[1], up[0], up[1], down.transpose(1, 0, 2)], axis=2)
    wqkv = np.concatenate([get("L0_attn_Wqkv"), get("L0_attn_lr_w")], axis=0).T
    wqkv = wqkv.reshape(DK, P, 3 * D + 3 * NH).transpose(1, 0, 2)
    wo = get("L0_attn_Wo").T.reshape(DK, P, D).transpose(1, 0, 2)
    w0, w1, w2 = get("L0_attn_w0"), get("L0_attn_w1"), get("L0_attn_w2")
    w02 = np.stack([w0.transpose(0, 2, 1), w2.transpose(0, 2, 1)], axis=2)
    w1s = np.stack([w1, w1.transpose(0, 2, 1)], axis=1)
    par = np.concatenate([
        get("L0_attn_q_norm_w"), get("L0_attn_k_norm_w"), get("L0_attn_qk_scale").T.reshape(-1),
        get("L0_attn_qk_offset").T.reshape(-1), get("L0_attn_ttt_norm_w"), get("L0_attn_lr_b")])
    idx = get("L0_ffn_topk_idx").reshape(2, P, TOPK).transpose(1, 0, 2)
    topw = get("L0_ffn_topk_weight").reshape(2, P, TOPK).transpose(1, 0, 2)
    inv_freq = (1.0 / f32(500000.0) ** (np.arange(0, HD, 2, dtype=f32) / f32(HD))).astype(f32)
    ang = (np.arange(S, dtype=f32)[:, None] * inv_freq[None, :]).astype(f32)
    cos, sin = np.cos(ang).astype(f32), np.sin(ang).astype(f32)
    trig = np.stack([cos, -sin, sin], axis=1).reshape(2, P, 3, 8).transpose(1, 0, 2, 3).reshape(P, 48)
    part = np.arange(P)
    parity = (part // HD) % 2
    small = np.concatenate([trig, np.stack([parity == 0, parity == 1], 1), np.tile(np.arange(E), (P, 1))], axis=1)
    qi, kj = part[:, None], part[None, :]
    causal = np.where(kj <= qi, 0.0, MASKED)
    before = np.where(kj > qi, 0.0, MASKED)
    mask = np.concatenate([causal, before, causal], axis=1)
    quarter = np.uint16(0x3E80)
    expand = np.tile(quarter * (np.arange(E)[:, None] == (np.arange(E * I) // I)[None, :]), (3, 1)).astype(np.uint16)

    arrays = {
        "x": get("L0_attn_hidden_states"), "wff": wff, "wqkv": wqkv, "wo": wo, "w02": w02, "w1": w1s, "idx": idx,
        "topw": topw, "par": par, "ident": np.eye(P), "mask": mask, "small": small, "expand": expand,
    }
    ints = {"idx", "expand"}
    arrays = {k: np.ascontiguousarray(v if k in ints else v.astype(f32, copy=False)) for k, v in arrays.items()}
    nc = bacc.Bacc("TRN2", target_bir_lowering=False, num_devices=1)
    aps = [nc.dram_tensor(k + "_dram", v.shape, mybir.dt.from_np(v.dtype), kind="ExternalInput").ap() for k, v in arrays.items()]
    aps.append(nc.dram_tensor("out", (B, S, D), F32, kind="ExternalOutput").ap())
    build(nc, *aps)
    r = run_bass_kernel_spmd(nc, [{k + "_dram": v for k, v in arrays.items()}], core_ids=[0])
    return r.results[0]["out"]
```

```python
import math
from contextlib import ExitStack

import concourse.bass as bass
from concourse import mybir

F32 = mybir.dt.float32
BF16 = mybir.dt.bfloat16
I32 = mybir.dt.int32
ALU = mybir.AluOpType
ACT = mybir.ActivationFunctionType
AX = mybir.AxisListType

P = 128
B, S, D = 4, 256, 256
H, HD = 16, 16
NH, FD = 4, 64
E, I, TOPK = 16, 176, 4
DK = D // P
FT = E * I // P
NU = FT // 2
NPAIR = NH // 2
VPAD = 16
NPAR = 6 * D + FD + 3 * NH
MASKED = -1.0e30
BASE_LR_INV = 0.001 + math.log(-math.expm1(-0.001))
ORDER = [(1, 0), (1, 1), (0, 0), (2, 0), (0, 1), (2, 1), (3, 0), (3, 1)]
NT = len(ORDER)


def unit_heads(t, u):
    return [2 * u, 2 * u + 1, 8 + 2 * u, 9 + 2 * u] if t == 0 else [2 * u, 2 * u + 1]


KV_SLOT = {1: 0, 0: 1, 2: 0, 3: 1}
UNITS = [4 if t == 0 else 8 for _, t in ORDER]
UBASE = [sum(UNITS[:n]) for n in range(NT + 1)]


STEPS = {
    "pe": """
        C CX CX G1 CX CX F P1 CX P2 CX CX F F CX D CX CX CX F D D F P3 D P4 F P1 PR F D S P2 S T Ta D V T F S V
        F D S F T F T Tb D V V G1 D PR Tc1 D S F Tc2 S T P3 D S P4 T V O1 S T O2 V P1 D O3 S P2 S T Ta S V F T V
        F S T Tb T V V F T Tc1 PR V V D D P3 D Tc2 S P4 F O1 S F T S P1 O2 D O3 S P2 T V D Ta F T F V V T F V F
        Tb D D PR Tc1 D F Tc2 S P3 D S P4 D O1 S T O2 S P1 T O3 T P2 V T G1 V Ta V V F F Tb F D D Tc1 F PR P3 D
        P4 Tc2 S O1 F T F S V P1 D O2 S T O3 S P2 S T Ta S T V V D V T F F D S T Tb S T V V Tc1 F PR T P3 V F
        Tc2 S V P4 S O1 T D P1 S O2 T V O3 S P2 T S Ta S T V V D T F D V D S Tb G1 T S V Tc1 V T F D PR T P3 V F
        Tc2 P4 S V F O1 S P1 T O2 D O3 S P2 S T Ta V F F T V D D T V F F V Tb D D D PR Tc1 F Tc2 S P3 F S P4 T D
        O1 S T O2 V S O3 T S Ta S T F V V D V T D S T Tb V S D Tc1 T V F Tc2 T V V O1 D O2 O3""",
    "act": """
        CX CX G1 CX CX F P1 CX P2 CX CX F F CX E CX CX N CX F F P3 P4 P1 F F S P2 S Ta E T F N S F S F F T G1
        Tc1 S F Tc2 P3 S P4 T S O2 P1 S S P2 Ta S T F N E F S T S F T Tc1 P3 Tc2 P4 S F S F P1 O2 S P2 S T Ta F
        E F N T F F Tc1 F Tc2 P3 S P4 S O2 S P1 T S P2 Ta T G1 E F N F F Tc1 F P3 P4 Tc2 S F F P1 S O2 T S S P2
        S Ta T E N S F F T S S Tc1 F T P3 F Tc2 P4 S S P1 O2 T S S P2 S Ta E T N F S G1 S T Tc1 S F T P3 F Tc2
        P4 S F P1 O2 S S P2 S Ta T F E F N T F F Tc1 F Tc2 P3 S F P4 S T O2 S S S Ta T S F S T Tc1 S F Tc2 T O2""",
    "dve": """
        G C G G1 L G1 P1 L P1 R F P2 K F F Q N F N2 F F PR F S S T P2 Q Ta N S K F S F T F F Tb O0 PR N2 Tc1 S F
        Tc2 S T FE Tc3 S L O1 P1 S L O3 T P1 S S P2 Ta Q N S T F F K S Tb T N2 F Tc1 PR O0 S Tc2 F S Tc3 O1 S T
        F O3 S P2 Q Ta N T K F F O0 F Tb F N2 PR Tc1 F Tc2 S Tc3 S FE O1 L S T P1 L S P1 L O3 G G1 T P2 Ta Q O0
        K N F F Tb N2 F Tc1 PR F Tc2 S T F Tc3 O1 S P1 L F S O3 S S T P2 Ta Q N S T K F S Tb F S N2 T Tc1 PR Tc2
        S O0 Tc3 S O1 T F S F P1 O3 S G G1 T S P2 Ta Q N S T K F S Tb N2 S Tc1 T PR FE F F Tc2 S O0 Tc3 O1 S T F
        O3 S S P2 Q Ta N T K F F O0 F Tb N2 F PR Tc1 F Tc2 S Tc3 F S T O1 S S O3 T S Ta S T F S Tb S Tc1 T Tc2 F
        O0 Tc3 O1 FE O3""",
    "pool": """
        R G L G L P2 F Q F F N F NR F K F F P2 Q NR Ta F N F F K F Tc2 F L L P2 Q Ta N NR F F F K Tc2 F F P2 Q
        NR N Ta F F F K F Tc2 F L L L G P2 Q Ta N F F NR F K Tc2 F F F L P2 Q Ta N NR K Tc2 F F F F G P2 Q Ta N
        F NR K Tc2 F F F P2 Q NR N Ta F F F K F Tc2 F F Ta F Tc2 F""",
}


def number(engine, kinds):
    units = [(n, u) for n in range(NT) for u in range(UNITS[n])]
    ffn_units = [(j, i) for j in range(4) for i in range(NU)]
    index = {"S": units, "T": units, "V": units, "F": ffn_units, "D": ffn_units}
    if engine == "dve":
        index["T"] = units[0::2]
    elif engine == "act":
        index["T"] = units[1::2]
    seen = {}
    steps = []
    for kind in kinds.split():
        i = seen.get(kind, 0)
        seen[kind] = i + 1
        steps.append((kind, *index[kind][i]) if kind in index else (kind, i))
    return steps


SCHEDULE = {engine: number(engine, kinds) for engine, kinds in STEPS.items()}


def build(nc, x_d, wff_d, wqkv_d, wo_d, w02_d, w1_d, idx_d, topw_d, par_d, ident_d, mask_d, small_d, expand_d,
          out_d):
    ctx = ExitStack()
    with ctx:
        def sb(name, shape, dt=F32):
            return ctx.enter_context(nc.sbuf_tensor(name, shape, dt))

        def bank(name, dt=F32, n=512):
            return ctx.enter_context(nc.psum_tensor(name, [P, n], dt))

        def sem(name):
            return ctx.enter_context(nc.semaphore(name))

        wff = sb("wff", [P, FT, 3 * D])
        wqkv = sb("wqkv", [P, DK, 3 * D + 3 * NH])
        wo = sb("wo", [P, DK, D])
        par = sb("par", [P, NPAR])
        ident = sb("ident", [P, P])
        small = sb("small", [P, 48 + 2 + E])
        identb = sb("identb", [P, P], BF16)
        mask = sb("mask", [P, 3 * P])
        cosw = sb("cosw", [P, 2, 512])
        sinw = sb("sinw", [P, 2, 512])
        halfc = sb("halfc", [P, 16])
        w02 = sb("w02", [P, 3, NPAIR, 2, 2 * FD])
        w1oh = sb("w1oh", [P, 3, NPAIR, 2 * FD])
        w1ho = sb("w1ho", [P, 3, NPAIR, 2 * FD])
        INIT = 2
        trig = small[:, 0:48].rearrange("p (t k d) -> p t k d", t=2, k=3)
        head_mask = small[:, 48:50]
        expert_no = small[:, 50:50 + E]
        xs = sb("xs", [P, B, 2, D])
        idx_i = sb("idx_i", [P, 2, TOPK], I32)
        idx_f = sb("idx_f", [P, 2, TOPK])
        topw = sb("topw", [P, 2, TOPK])
        coef1 = sb("coef1", [P, 2, TOPK, E])
        coef = sb("coef", [P, 2, E])
        coef_r = sb("coef_r", [P, 2, 2, E])
        coef3 = sb("coef3", [P, 2, 3 * E], BF16)
        coefT = sb("coefT", [3 * E, 2 * P], BF16)
        coefx = sb("coefx", [P, FT, 2 * P])
        fst = sb("fst", [P, 2, 6])
        fmv = sb("fmv", [P, 2, 2])
        fve = sb("fve", [P, 2])
        frs = sb("frs", [P, 2])
        fxT = sb("fxT", [P, 2, D])
        fth = sb("fth", [P, 2, D])
        fa = sb("fa", [P, D])
        fb = sb("fb", [P, 2, D])
        fxn = sb("fxn", [P, D])
        fh = sb("fh", [P, 3, D])
        lst = sb("lst", [P, 2, 6])
        lmv = sb("lmv", [P, 2, 2])
        lve = sb("lve", [P, 2])
        lrs = sb("lrs", [P, 2])
        xn = sb("xn", [P, D])
        xnT = sb("xnT", [P, DK, P])
        ssqk = sb("ssqk", [P, 2, 2])
        msqk = sb("msqk", [P, 2, 2])
        rqk = sb("rqk", [P, 2, 2])
        th = sb("th", [P, 3 * D])
        qks = sb("qks", [P, 2 * D])
        rp1 = sb("rp1", [P, 2 * D])
        rp2 = th[:, 0:2 * D]
        rope = qks
        s2 = sb("s2", [P, 2 * D])
        s2v = sb("s2v", [P, 2, D])
        f1 = rp1
        f2 = sb("f2", [P, 2 * D])
        sqs = sb("sqs", [P, 2 * D])
        sqf = sqs
        ss8 = sb("ss8", [P, 2 * NH])
        nrm = sb("nrm", [P, 2 * NH])
        inv8 = sb("inv8", [P, 3, 2 * NH])
        fn = sb("fn", [P, 2 * D])
        fT = sb("fT", [P, 4, P])
        fvT = sb("fvT", [P, NPAIR, P])
        z = sb("z", [P, 5, 3 * NH])
        ez = sb("ez", [P, 3 * NH])
        rz = sb("rz", [P, 3 * NH])
        lz = sb("lz", [P, 24, 3 * NH])
        lr = sb("lr", [P, 2, 3 * NH])
        lrh = sb("lrh", [P, 2, NH])
        qTm = sb("qTm", [P, 2, 2, 2, P])
        kT = sb("kT", [P, 2, 2, 2 * P])
        vS = sb("vS", [P, 2, 2, D + VPAD])
        nmax = sb("nmax", [P, 2, 4])
        pST = sb("pST", [P, 4, 512])
        pS, pT = pST[:, 0:2], pST[:, 2:4]
        expand = pST[:].rearrange("p a b -> p (a b)").bitcast(BF16)[0:3 * E, 0:FT * P]
        rsum = sb("rsum", [P, 2, H])
        rinv = sb("rinv", [P, H])
        oS = sb("oS", [P, 512])
        aS = sb("aS", [P, D])
        ta = sb("ta", [P, D])
        si = sb("si", [P, D])
        hid = sb("hid", [P, D])
        dhp = sb("dhp", [P, D])
        q1 = sb("q1", [P, D])
        dg = sb("dg", [P, D])
        dd = sb("dd", [P, NPAIR, 2, 2 * FD])
        vl = sb("vl", [P, D])
        sg, tq, sq2, tg, q3 = ta, ta, si, q1, q1
        hqT = sb("hqT", [P, NPAIR, P])
        sqo = sb("sqo", [P, D])
        ss4 = sb("ss4", [P, NH])
        ms4 = sb("ms4", [P, NH])
        r4 = sb("r4", [P, NH])
        tt = sb("tt", [P, D])
        ttw, yS = tt, tt
        yT = sb("yT", [P, DK, P])
        GU = [bank("GU0"), bank("GU1")]
        DN = bank("DN")
        SC = bank("SC")
        PT = bank("PT")
        OT = bank("OT")
        X = bank("X")
        Y = bank("Y")

        qknw, scl, off = par[:, 0:512], par[:, 512:1024], par[:, 1024:1536]
        ttw_w, lrb = par[:, 1536:1536 + FD], par[:, 1536 + FD:NPAR]

        l_x = [sem(f"l_x{b}") for b in range(B)]
        l_route, l_par, l_small, l_ident, l_mask = (sem(n) for n in ("l_route", "l_par", "l_small", "l_ident", "l_mask"))
        l_wqkv, l_wo, l_expand, l_init = (sem(n) for n in ("l_wqkv", "l_wo", "l_expand", "l_init"))
        l_wff = [sem(f"l_wff{i}") for i in range(FT // 2)]
        stored = sem("stored")
        zeroed, consts, trig_ready = sem("zeroed"), sem("consts"), sem("trig_ready")
        coef_ready, coefT_psum, coefT_ready, coefx_psum, coefx_ready = (
            sem(n) for n in ("coef_ready", "coefT_psum", "coefT_ready", "coefx_psum", "coefx_ready"))
        dve_chain, act_chain, pool_chain = sem("dve_chain"), sem("act_chain"), sem("pool_chain")
        fstats, frstd, fxn_ready, fxT_psum, fxT_ready = (sem(n) for n in ("fstats", "frstd", "fxn_ready", "fxT_psum", "fxT_ready"))
        gu_ready, fth_ready, gated, h_ready, down_done, ffn_added = (
            sem(n) for n in ("gu_ready", "fth_ready", "gated", "h_ready", "down_done", "ffn_added"))
        ln_stats, ln_rstd, xn_ready, xnT_psum, xnT_ready, qkv_ready = (
            sem(n) for n in ("ln_stats", "ln_rstd", "xn_ready", "xnT_psum", "xnT_ready", "qkv_ready"))
        ss_ready, rqk_ready, th_ready, silu_ready, qk_scaled, qkv_sb, ez_ready, rz_ready, lr_ready = (
            sem(n) for n in ("ss_ready", "rqk_ready", "th_ready", "silu_ready", "qk_scaled", "qkv_sb", "ez_ready",
                             "rz_ready", "lr_ready"))
        f_ready, rope_ready, sqf_ready, ss8_ready, nrm_ready, fn_ready = (
            sem(n) for n in ("f_ready", "rope_ready", "sqf_ready", "ss8_ready", "nrm_ready", "fn_ready"))
        fT_psum, qkT_psum, fT_ready, qkT_ready, fvT_psum, fvT_ready = (
            sem(n) for n in ("fT_psum", "qkT_psum", "fT_ready", "qkT_ready", "fvT_psum", "fvT_ready"))
        scores_ready, nmax_ready, exp_done, pT_psum, pT_ready, pv_done = (
            sem(n) for n in ("scores_ready", "nmax_ready", "exp_done", "pT_psum", "pT_ready", "pv_done"))
        oS_ready, o_psum, attn_ready, y_ready, yT_psum, yT_ready, wo_psum, x2_ready = (
            sem(n) for n in ("oS_ready", "o_psum", "attn_ready", "y_ready", "yT_psum", "yT_ready", "wo_psum", "x2_ready"))
        ta_psum, ta_ready, grads_ready, dd_ready, tb_psum, w_updated = (
            sem(n) for n in ("ta_psum", "ta_ready", "grads_ready", "dd_ready", "tb_psum", "w_updated"))
        gq_psum, tq_ready, hq_ready, oi_psum, sqo_ready, ss4_ready, r4_ready, tt_ready, ttw_ready = (
            sem(n) for n in ("gq_psum", "tq_ready", "hq_ready", "oi_psum", "sqo_ready", "ss4_ready", "r4_ready",
                             "tt_ready", "ttw_ready"))

        def heads(ap, n, w):
            return ap.rearrange("p (n w) -> p n w", n=n, w=w)

        def spread(ap, n, w):
            return ap.unsqueeze(2).broadcast_to([P, n, w])

        def w_old(n):
            b, t = ORDER[n]
            return INIT if t == 0 else KV_SLOT[b]

        block = ctx.enter_context(nc.Block())

        @block.sync
        def _(sp):
            sp.dma_start(xs[:, 0], x_d[0].rearrange("(t p) d -> p t d", p=P)).then_inc(l_x[0], 16)
            sp.dma_start(ident[:], ident_d).then_inc(l_ident, 16)
            sp.dma_start(small[:], small_d).then_inc(l_small, 16)
            sp.dma_start(idx_i[:], idx_d).then_inc(l_route, 16)
            sp.dma_start(topw[:], topw_d).then_inc(l_route, 16)
            sp.dma_start(wff[:, 0:2, :], wff_d[:, 0:2, :]).then_inc(l_wff[0], 16)
            sp.dma_start(expand, expand_d.bitcast(BF16)).then_inc(l_expand, 16)
            sp.dma_start(xs[:, 1], x_d[1].rearrange("(t p) d -> p t d", p=P)).then_inc(l_x[1], 16)
            sp.dma_start(wqkv[:], wqkv_d).then_inc(l_wqkv, 16)
            sp.dma_start(par[:], par_d.partition_broadcast(P)).then_inc(l_par, 16)
            sp.dma_start(mask[:], mask_d).then_inc(l_mask, 16)
            for i in range(1, FT // 2):
                sp.dma_start(wff[:, 2 * i:2 * i + 2, :], wff_d[:, 2 * i:2 * i + 2, :]).then_inc(l_wff[i], 16)
                if i == 3:
                    sp.wait_ge(zeroed, 3)
                    for h in range(NH):
                        p, a = h // 2, h % 2
                        rows = slice(FD * a, FD * a + FD)
                        sp.dma_start(w02[rows, INIT, p, :, FD * a:FD * a + FD], w02_d[h]).then_inc(l_init, 16)
                        sp.dma_start(w1oh[rows, INIT, p, FD * a:FD * a + FD], w1_d[h, 0]).then_inc(l_init, 16)
                        sp.dma_start(w1ho[rows, INIT, p, FD * a:FD * a + FD], w1_d[h, 1]).then_inc(l_init, 16)
                if i == 2:
                    sp.dma_start(wo[:], wo_d).then_inc(l_wo, 16)
                    for b in (2, 3):
                        sp.dma_start(xs[:, b], x_d[b].rearrange("(t p) d -> p t d", p=P)).then_inc(l_x[b], 16)
            for n, (b, t) in enumerate(ORDER):
                if b:
                    sp.wait_ge(x2_ready, n + 1)
                    sp.dma_start(out_d[b, t * P:(t + 1) * P, :], xs[:, b, t]).then_inc(stored, 16)
            for t in range(2):
                sp.wait_ge(ffn_added, 3 + t)
                sp.dma_start(out_d[0, t * P:(t + 1) * P, :], xs[:, 0, t]).then_inc(stored, 16)
            sp.wait_ge(stored, 16 * 2 * B)

        @block.gpsimd
        def _(pool):
            links = [0]

            def link(ins):
                links[0] += 1
                ins.then_inc(pool_chain, 1)
                pool.wait_ge(pool_chain, links[0])

            pool.memset(halfc[:, 0:8], -0.5)
            link(pool.memset(halfc[:, 8:16], 0.5))
            for step in SCHEDULE["pool"]:
                kind, n = step[0], step[1] if len(step) > 1 else 0
                if kind == "R":
                    pool.memset(w02[:], 0.0).then_inc(zeroed, 1)
                    pool.memset(w1oh[:], 0.0).then_inc(zeroed, 1)
                    pool.memset(w1ho[:], 0.0).then_inc(zeroed, 1)
                    pool.memset(vS[:, :, :, D:D + VPAD], 0.0).then_inc(consts, 1)
                elif kind == "L":
                    s = n % 2
                    pool.wait_ge(ln_stats, n + 1)
                    link(pool.tensor_scalar(lve[:, s:s + 1], lmv[:, s, 1:2], 1e-5, None, ALU.add))
                    pool.tensor_tensor(lrs[:, s:s + 1], lve[:, s:s + 1], halfc[:, 0:1], ALU.pow).then_inc(ln_rstd, 1)
                elif kind == "G":
                    pool.wait_ge(fstats, n + 1)
                    t = n % 2
                    link(pool.tensor_scalar(fve[:, t:t + 1], fmv[:, t, 1:2], 1e-5, None, ALU.add))
                    pool.tensor_tensor(frs[:, t:t + 1], fve[:, t:t + 1], halfc[:, 0:1], ALU.pow).then_inc(frstd, 1)
                elif kind == "F":
                    i = step[2]
                    m = n * NU + i
                    pool.wait_ge(gated, m + 1)
                    if m >= 3:
                        pool.wait_ge(down_done, m - 2)
                    if n == 0:
                        pool.wait_ge(coefx_ready, i + 1)
                    elif n == 1 and i == 0:
                        pool.wait_ge(coefx_ready, NU)
                    t = n % 2
                    pool.tensor_tensor(heads(fh[:, m % 3], 2, P), heads(fb[:, m % 2], 2, P),
                                       coefx[:, 2 * i:2 * i + 2, t * P:(t + 1) * P], ALU.mult).then_inc(h_ready, 1)
                elif kind == "P2":
                    s = n % 2
                    pool.wait_ge(ss_ready, n + 1)
                    link(pool.tensor_scalar(msqk[:, s], ssqk[:, s], 1.0 / D, 1e-6, ALU.mult, ALU.add))
                    pool.tensor_tensor(rqk[:, s], msqk[:, s], halfc[:, 0:2], ALU.pow).then_inc(rqk_ready, 1)
                elif kind == "Q":
                    pool.wait_ge(silu_ready, n + 1)
                    if n >= 1:
                        pool.wait_ge(fn_ready, n)
                        pool.wait_ge(rope_ready, n)
                    link(pool.tensor_tensor(f1[:], s2[:], scl, ALU.mult))
                    pool.tensor_tensor(f2[:], f1[:], off, ALU.add).then_inc(f_ready, 1)
                elif kind == "N":
                    pool.wait_ge(ss8_ready, n + 1)
                    pool.tensor_tensor(nrm[:], ss8[:], halfc[:, 8:16], ALU.pow).then_inc(nrm_ready, 1)
                elif kind == "NR":
                    t = ORDER[n][1]
                    pool.wait_ge(qk_scaled, n + 1)
                    pool.wait_ge(f_ready, n + 1)
                    if n == 0:
                        pool.wait_ge(trig_ready, 1)
                    pool.tensor_tensor(rp1[:], qks[:], cosw[:, t], ALU.mult)
                    src = qks[:].rearrange("p (h k d) -> p h k d", k=2, d=8)
                    dst = rp2.rearrange("p (h k d) -> p h k d", k=2, d=8)
                    tab = sinw[:, t].rearrange("p (h k d) -> p h k d", k=2, d=8)
                    pool.tensor_tensor(dst[:, :, 0], src[:, :, 1], tab[:, :, 0], ALU.mult)
                    link(pool.tensor_tensor(dst[:, :, 1], src[:, :, 0], tab[:, :, 1], ALU.mult))
                    pool.tensor_tensor(rope[:], rp1[:], rp2, ALU.add).then_inc(rope_ready, 1)
                elif kind == "K":
                    s = n % 2
                    pool.wait_ge(rz_ready, n + 1)
                    link(pool.tensor_tensor(lz[:, 0], ez[:], rz[:], ALU.mult))
                    link(pool.tensor_tensor(lz[:, 1], lz[:, 0], lz[:, 0], ALU.mult))
                    link(pool.tensor_scalar(lz[:, 2], lz[:, 1], 1 / 17, 1 / 15, ALU.mult, ALU.add))
                    for j, c in enumerate([13, 11, 9, 7, 5, 3, 1]):
                        link(pool.tensor_tensor(lz[:, 3 + 2 * j], lz[:, 2 + 2 * j], lz[:, 1], ALU.mult))
                        link(pool.tensor_scalar(lz[:, 4 + 2 * j], lz[:, 3 + 2 * j], 1 / c, None, ALU.add))
                    link(pool.tensor_tensor(lz[:, 17], lz[:, 16], lz[:, 0], ALU.mult))
                    link(pool.tensor_scalar(lz[:, 18], lz[:, 17], 2.0, None, ALU.mult))
                    link(pool.tensor_tensor(lr[:, s], lz[:, 18], z[:, 2], ALU.add))
                    pool.tensor_scalar(lrh[:, s], lr[:, s, NH:2 * NH], 0.5, None, ALU.mult).then_inc(lr_ready, 1)
                elif kind == "Ta":
                    s = n % 2
                    pool.wait_ge(grads_ready, n + 1)
                    pool.wait_ge(lr_ready, n + 1)
                    if n >= 1:
                        pool.wait_ge(tb_psum, n)
                    for p in range(NPAIR):
                        cols, hs = slice(p * P, (p + 1) * P), slice(2 * p, 2 * p + 2)
                        pool.tensor_tensor(heads(dd[:, p, 0], 2, FD), heads(dg[:, cols], 2, FD),
                                           spread(lr[:, s, 0:NH][:, hs], 2, FD), ALU.mult)
                        pool.tensor_tensor(heads(dd[:, p, 1], 2, FD), heads(dhp[:, cols], 2, FD),
                                           spread(lr[:, s, 2 * NH:3 * NH][:, hs], 2, FD), ALU.mult)
                    pool.tensor_tensor(heads(vl[:], NH, FD), heads(s2v[:, s], NH, FD),
                                       spread(lrh[:, s], NH, FD), ALU.mult).then_inc(dd_ready, 1)
                elif kind == "Tc2":
                    pool.wait_ge(ss4_ready, n + 1)
                    link(pool.tensor_scalar(ms4[:], ss4[:], 1.0 / FD, 1e-6, ALU.mult, ALU.add))
                    pool.tensor_tensor(r4[:], ms4[:], halfc[:, 0:NH], ALU.pow).then_inc(r4_ready, 1)

        @block.scalar
        def _(act):
            links = [0]

            def link(ins):
                links[0] += 1
                ins.then_inc(act_chain, 1)
                act.wait_ge(act_chain, links[0])

            for step in SCHEDULE["act"]:
                kind, n = step[0], step[1] if len(step) > 1 else 0
                if kind == "CX":
                    act.wait_ge(coefx_psum, n + 1)
                    act.activation(coefx[:, 2 * n:2 * n + 2], heads((SC, PT)[n % 2][:], 2, D), ACT.Copy)\
                       .then_inc(coefx_ready, 1)
                elif kind == "G1":
                    act.wait_ge(fxT_psum, n + 1)
                    if n >= 2:
                        act.wait_ge(gu_ready, (n - 1) * NU)
                    act.activation(fxT[:, n % 2], GU[(n * NU + 1) % 2][:, 0:D], ACT.Copy).then_inc(fxT_ready, 1)
                elif kind == "F":
                    m = n * NU + step[2]
                    act.wait_ge(gu_ready, m + 1)
                    if m >= 2:
                        act.wait_ge(gated, m - 1)
                    act.activation(fth[:, m % 2], GU[m % 2][:, 0:D], ACT.Tanh, scale=0.5).then_inc(fth_ready, 1)
                elif kind == "P1":
                    act.wait_ge(xnT_psum, n + 1)
                    if n >= 1:
                        act.wait_ge(qkv_ready, n)
                    act.activation(xnT[:], heads(X[:, 0:D], DK, P), ACT.Copy).then_inc(xnT_ready, 1)
                elif kind == "P2":
                    (b, t), s = ORDER[n], n % 2
                    act.wait_ge(qkv_ready, n + 1)
                    if n >= 1:
                        act.wait_ge(qkT_psum, n)
                    act.activation(qks[:], X[:], ACT.Copy)
                    act.activation(vS[:, KV_SLOT[b], t, 0:D], Y[:, 0:D], ACT.Copy)
                    if n >= 1:
                        act.wait_ge(lr_ready, n)
                    act.activation(z[:, 4], Y[:, D:D + 3 * NH], ACT.Copy).then_inc(qkv_sb, 1)
                    act.wait_ge(qkv_sb, n + 1)
                    link(act.activation(sqs[:, 0:D], qks[:, 0:D], ACT.Square, accum_out=ssqk[:, s, 0:1]))
                    act.activation(sqs[:, D:2 * D], qks[:, D:2 * D], ACT.Square, accum_out=ssqk[:, s, 1:2])\
                       .then_inc(ss_ready, 1)
                    if n >= 1:
                        act.wait_ge(rope_ready, n)
                    act.activation(th[:, 0:512], qks[:], ACT.Tanh, scale=0.5)
                    act.activation(th[:, 512:768], vS[:, KV_SLOT[b], t, 0:D], ACT.Tanh, scale=0.5).then_inc(th_ready, 1)
                elif kind == "E":
                    act.wait_ge(silu_ready, n + 1)
                    act.activation(ez[:], z[:, 1], ACT.Exp, scale=-1.0).then_inc(ez_ready, 1)
                elif kind == "N":
                    act.wait_ge(f_ready, n + 1)
                    act.activation(sqf[:], f2[:], ACT.Square).then_inc(sqf_ready, 1)
                elif kind == "P3":
                    act.wait_ge(fT_psum, n + 1)
                    if n >= 1:
                        act.wait_ge(gq_psum, n)
                    act.activation(fT[:], heads(X[:], 4, P), ACT.Copy).then_inc(fT_ready, 1)
                elif kind == "P4":
                    act.wait_ge(fvT_psum, n + 1)
                    if n >= 1:
                        act.wait_ge(ta_psum, n)
                    act.activation(fvT[:], heads(X[:, 0:D], NPAIR, P), ACT.Copy, scale=0.5).then_inc(fvT_ready, 1)
                elif kind == "S":
                    u, t, s = step[2], ORDER[n][1], n % 2
                    q = UBASE[n] + u
                    nh = 4 if t == 0 else 2
                    w = 512 // nh
                    act.wait_ge(nmax_ready, q + 1)
                    if q >= 2:
                        act.wait_ge(pT_psum, q - 1)
                    for a, h in enumerate(unit_heads(t, u)):
                        ins = act.activation(pS[:, q % 2, a * w:(a + 1) * w], pS[:, q % 2, a * w:(a + 1) * w], ACT.Exp,
                                             scale=-1.0, bias=nmax[:, q % 2, a:a + 1], accum_out=rsum[:, s, h:h + 1])
                    ins.then_inc(exp_done, 1)
                elif kind == "T":
                    q = UBASE[n] + step[2]
                    if q % 2:
                        act.wait_ge(pT_psum, q + 1)
                        act.wait_ge(pv_done, q - 1)
                        act.activation(pT[:, q % 2], PT[:], ACT.Copy).then_inc(pT_ready, 1)
                elif kind == "Ta":
                    act.wait_ge(ta_psum, n + 1)
                    gate = X[:].rearrange("p (h k d) -> p h k d", h=NPAIR, k=2)[:, :, 0]
                    act.activation(heads(ta[:], NPAIR, P), gate, ACT.Tanh, scale=0.5).then_inc(ta_ready, 1)
                elif kind == "Tc1":
                    act.wait_ge(gq_psum, n + 1)
                    gate = X[:].rearrange("p (h k c) -> p h k c", h=NPAIR, k=2)[:, :, 0]
                    act.activation(heads(tq[:], NPAIR, P), gate, ACT.Tanh, scale=0.5).then_inc(tq_ready, 1)
                elif kind == "Tc2":
                    act.wait_ge(oi_psum, n + 1)
                    act.activation(sqo[:], Y[:, 0:D], ACT.Square).then_inc(sqo_ready, 1)
                elif kind == "O2":
                    act.wait_ge(yT_psum, n + 1)
                    act.activation(yT[:], heads(Y[:, 0:D], DK, P), ACT.Copy).then_inc(yT_ready, 1)

        @block.vector
        def _(dve):
            links = [0]

            def link(ins):
                links[0] += 1
                ins.then_inc(dve_chain, 1)
                dve.wait_ge(dve_chain, links[0])

            for step in SCHEDULE["dve"]:
                kind, n = step[0], step[1] if len(step) > 1 else 0
                if kind == "C":
                    dve.wait_ge(l_ident, 16)
                    dve.tensor_copy(identb[:], ident[:])
                    dve.wait_ge(l_route, 32)
                    dve.wait_ge(l_small, 16)
                    link(dve.tensor_copy(idx_f[:], idx_i[:]))
                    for t in range(2):
                        for k in range(TOPK):
                            last = dve.tensor_scalar(coef1[:, t, k], expert_no, idx_f[:, t, k:k + 1],
                                                     topw[:, t, k:k + 1], ALU.is_equal, ALU.mult)
                    link(last)
                    link(dve.tensor_reduce(coef[:], coef1[:].rearrange("p t k e -> p t e k"), AX.X, ALU.add))
                    link(dve.tensor_copy(coef3[:, :, 0:E], coef[:]))
                    link(dve.tensor_tensor(coef_r[:, 0], coef[:], coef3[:, :, 0:E], ALU.subtract))
                    link(dve.tensor_copy(coef3[:, :, E:2 * E], coef_r[:, 0]))
                    link(dve.tensor_tensor(coef_r[:, 1], coef_r[:, 0], coef3[:, :, E:2 * E], ALU.subtract))
                    dve.tensor_copy(coef3[:, :, 2 * E:3 * E], coef_r[:, 1]).then_inc(coef_ready, 1)
                    dve.wait_ge(coefT_psum, 1)
                    dve.tensor_copy(coefT[:], OT[:].bitcast(BF16)[0:3 * E, 0:2 * P]).then_inc(coefT_ready, 1)
                elif kind == "R":
                    dve.wait_ge(l_par, 16)
                    dve.wait_ge(l_small, 16)
                    link(dve.tensor_scalar(qknw[:, 0:D], qknw[:, 0:D], HD ** -0.5, None, ALU.mult))
                    link(dve.tensor_scalar(scl, scl, 0.5, None, ALU.mult))
                    link(dve.tensor_scalar(lrb, lrb, BASE_LR_INV, None, ALU.add))
                    nw = qknw.rearrange("p (h k d) -> p h k d", k=2, d=8)
                    for t in range(2):
                        co = cosw[:, t].rearrange("p (h k d) -> p h k d", k=2, d=8)
                        si_ = sinw[:, t].rearrange("p (h k d) -> p h k d", k=2, d=8)
                        for k in range(2):
                            def angle(a):
                                return trig[:, t, a].unsqueeze(1).broadcast_to([P, 2 * H, 8])
                            dve.tensor_tensor(co[:, :, k], nw[:, :, k], angle(0), ALU.mult)
                            last = dve.tensor_tensor(si_[:, :, k], nw[:, :, 1 - k], angle(1 + k), ALU.mult)
                    last.then_inc(trig_ready, 1)
                elif kind == "L":
                    (b, t), s = ORDER[n], n % 2
                    dve.wait_ge(l_x[b], 16)
                    if b == 0:
                        dve.wait_ge(ffn_added, t + 1)
                    link(dve.bn_stats(lst[:, s], xs[:, b, t]))
                    dve.bn_aggr(lmv[:, s], lst[:, s]).then_inc(ln_stats, 1)
                elif kind == "G":
                    t = n % 2
                    dve.wait_ge(l_x[0], 16)
                    if n >= 2:
                        dve.wait_ge(x2_ready, ORDER.index((0, t)) + 1)
                    link(dve.bn_stats(fst[:, t], xs[:, 0, t]))
                    dve.bn_aggr(fmv[:, t], fst[:, t]).then_inc(fstats, 1)
                elif kind == "G1":
                    t = n % 2
                    dve.wait_ge(frstd, n + 1)
                    if n:
                        dve.wait_ge(fxT_psum, n)
                    dve.tensor_scalar(fxn[:], xs[:, 0, t], fmv[:, t, 0:1], frs[:, t:t + 1], ALU.subtract, ALU.mult)\
                       .then_inc(fxn_ready, 1)
                elif kind == "F":
                    m = n * NU + step[2]
                    s, G = m % 2, GU[m % 2]
                    dve.wait_ge(fth_ready, m + 1)
                    if m >= 1:
                        dve.wait_ge(gated, m)
                    if m >= 2:
                        dve.wait_ge(h_ready, m - 1)
                    link(dve.scalar_tensor_tensor(fa[:], fth[:, s], 1.0, G[:, 0:D], ALU.add, ALU.mult))
                    dve.tensor_tensor(fb[:, s], fa[:], G[:, D:2 * D], ALU.mult).then_inc(gated, 1)
                elif kind == "FE":
                    dve.wait_ge(down_done, (n + 1) * NU)
                    x0 = xs[:, 0, n % 2]
                    dve.tensor_tensor(x0, x0, DN[:, 0:D], ALU.add).then_inc(ffn_added, 1)
                elif kind == "P1":
                    (b, t), s = ORDER[n], n % 2
                    dve.wait_ge(ln_rstd, n + 1)
                    if n >= 1:
                        dve.wait_ge(xnT_psum, n)
                    dve.tensor_scalar(xn[:], xs[:, b, t], lmv[:, s, 0:1], lrs[:, s:s + 1],
                                      ALU.subtract, ALU.mult).then_inc(xn_ready, 1)
                elif kind == "P2":
                    (b, t), s = ORDER[n], n % 2
                    dve.wait_ge(th_ready, n + 1)
                    dve.wait_ge(l_par, 16)
                    if n >= 1:
                        dve.wait_ge(f_ready, n)
                    dve.scalar_tensor_tensor(s2[:], th[:, 0:512], 1.0, qks[:], ALU.add, ALU.mult)
                    dve.scalar_tensor_tensor(s2v[:, s], th[:, 512:768], 1.0, vS[:, KV_SLOT[b], t, 0:D],
                                             ALU.add, ALU.mult)
                    link(dve.tensor_tensor(z[:, 0], z[:, 4], lrb, ALU.add))
                    dve.tensor_scalar(z[:, 2], z[:, 0], 0.0, None, ALU.max)
                    link(dve.tensor_scalar(z[:, 3], z[:, 0], -1.0, None, ALU.mult))
                    dve.tensor_tensor(z[:, 1], z[:, 0], z[:, 3], ALU.max).then_inc(silu_ready, 1)
                elif kind == "Q":
                    s = n % 2
                    dve.wait_ge(rqk_ready, n + 1)
                    dve.wait_ge(silu_ready, n + 1)
                    dve.tensor_scalar(qks[:, 0:D], qks[:, 0:D], rqk[:, s, 0:1], None, ALU.mult)
                    dve.tensor_scalar(qks[:, D:2 * D], qks[:, D:2 * D], rqk[:, s, 1:2], None, ALU.mult)\
                       .then_inc(qk_scaled, 1)
                elif kind == "N":
                    dve.wait_ge(sqf_ready, n + 1)
                    dve.tensor_reduce(ss8[:], heads(sqf[:], 2 * NH, FD), AX.X, ALU.add).then_inc(ss8_ready, 1)
                elif kind == "K":
                    dve.wait_ge(ez_ready, n + 1)
                    link(dve.tensor_scalar(z[:, 3], ez[:], 2.0, None, ALU.add))
                    dve.reciprocal(rz[:], z[:, 3]).then_inc(rz_ready, 1)
                elif kind == "N2":
                    s = n % 2
                    dve.wait_ge(nrm_ready, n + 1)
                    link(dve.tensor_scalar(inv8[:, 0], nrm[:], 1e-12, None, ALU.add))
                    link(dve.reciprocal(inv8[:, 1], inv8[:, 0]))
                    if n >= 1:
                        dve.wait_ge(tb_psum, n)
                    dve.tensor_tensor(heads(fn[:], 2 * NH, FD), heads(f2[:], 2 * NH, FD),
                                      spread(inv8[:, 1], 2 * NH, FD), ALU.mult).then_inc(fn_ready, 1)
                elif kind == "PR":
                    (b, t), s = ORDER[n], n % 2
                    dve.wait_ge(qkT_psum, n + 1)
                    dve.tensor_copy(kT[:, KV_SLOT[b], :, t * P:(t + 1) * P], heads(Y[:, D:2 * D], 2, P))
                    for k in range(2):
                        last = dve.tensor_scalar(qTm[:, s, k], heads(Y[:, 0:D], 2, P), head_mask[:, k:k + 1], None,
                                                 ALU.mult)
                    last.then_inc(qkT_ready, 1)
                elif kind == "S":
                    nh = 4 if ORDER[n][1] == 0 else 2
                    q = UBASE[n] + step[2]
                    w, t = 512 // nh, ORDER[n][1]
                    dve.wait_ge(scores_ready, q + 1)
                    if q == 0:
                        dve.wait_ge(l_mask, 16)
                    if q >= 2:
                        dve.wait_ge(pT_psum, q - 1)
                    for a in range(nh):
                        last = dve.tensor_tensor_reduce(pS[:, q % 2, a * w:(a + 1) * w], SC[:, a * w:(a + 1) * w],
                                                        mask[:, t * P:t * P + w], -1.0, -MASKED, ALU.add, ALU.min,
                                                        nmax[:, q % 2, a:a + 1])
                    last.then_inc(nmax_ready, 1)
                elif kind == "T":
                    q = UBASE[n] + step[2]
                    if q % 2 == 0:
                        dve.wait_ge(pT_psum, q + 1)
                        if q >= 2:
                            dve.wait_ge(pv_done, q - 1)
                        dve.tensor_copy(pT[:, q % 2], PT[:]).then_inc(pT_ready, 1)
                elif kind == "O0":
                    dve.wait_ge(pv_done, UBASE[n + 1])
                    if n >= 1:
                        dve.wait_ge(attn_ready, n)
                    dve.reciprocal(rinv[:], rsum[:, n % 2])
                    dve.tensor_copy(oS[:], OT[:]).then_inc(oS_ready, 1)
                elif kind == "O1":
                    dve.wait_ge(o_psum, n + 1)
                    dve.wait_ge(oS_ready, n + 1)
                    dve.wait_ge(ttw_ready, n + 1)
                    o = X[:].rearrange("p (h w) -> p h w", w=2 * HD)[:, :, 0:HD]
                    dve.tensor_tensor(heads(aS[:], H, HD), o, spread(rinv[:], H, HD), ALU.mult)\
                       .then_inc(attn_ready, 1)
                    dve.wait_ge(attn_ready, n + 1)
                    dve.tensor_tensor(yS[:], aS[:], ttw[:], ALU.add).then_inc(y_ready, 1)
                elif kind == "O3":
                    b, t = ORDER[n]
                    dve.wait_ge(wo_psum, n + 1)
                    dve.tensor_tensor(xs[:, b, t], xs[:, b, t], X[:, 0:D], ALU.add).then_inc(x2_ready, 1)
                elif kind == "Ta":
                    g = X[:].rearrange("p (h k d) -> p h k d", h=NPAIR, k=2)
                    gate, up, dh = g[:, :, 0], g[:, :, 1], heads(Y[:, 0:D], NPAIR, P)
                    dve.wait_ge(ta_ready, n + 1)
                    if n >= 1:
                        dve.wait_ge(dd_ready, n)
                        dve.wait_ge(tb_psum, n)
                    link(dve.tensor_scalar(sg[:], ta[:], 0.5, 0.5, ALU.mult, ALU.add))
                    link(dve.tensor_tensor(heads(si[:], NPAIR, P), heads(sg[:], NPAIR, P), gate, ALU.mult))
                    dve.tensor_tensor(heads(hid[:], NPAIR, P), heads(si[:], NPAIR, P), up, ALU.mult)
                    dve.tensor_tensor(heads(dhp[:], NPAIR, P), heads(si[:], NPAIR, P), dh, ALU.mult)
                    link(dve.tensor_tensor(heads(q1[:], NPAIR, P), gate, heads(si[:], NPAIR, P), ALU.subtract))
                    link(dve.scalar_tensor_tensor(q3[:], q1[:], 1.0, sg[:], ALU.add, ALU.mult))
                    link(dve.tensor_tensor(heads(tg[:], NPAIR, P), heads(q3[:], NPAIR, P), dh, ALU.mult))
                    dve.tensor_tensor(heads(dg[:], NPAIR, P), heads(tg[:], NPAIR, P), up, ALU.mult).then_inc(grads_ready, 1)
                elif kind == "Tb":
                    old, new, t = w_old(n), KV_SLOT[ORDER[n][0]], ORDER[n][1]
                    dve.wait_ge(tb_psum, n + 1)
                    dve.wait_ge(l_init, 16 * 3 * NH)
                    dve.wait_ge(zeroed, 3)
                    for a in range(2):
                        rows = slice(FD * a, FD * a + FD)
                        c1 = slice(FD * a, FD * (a + 1))
                        dve.tensor_tensor(w02[rows, new, :, :, c1], w02[rows, old, :, :, c1],
                                          X[rows, :].rearrange("p (n k c) -> p n k c", n=NPAIR, k=2)[:, :, :, c1],
                                          ALU.add)
                        if t == 0:
                            dve.tensor_tensor(w1oh[rows, new, :, c1], w1oh[rows, old, :, c1],
                                              heads(Y[rows, D:2 * D], NPAIR, 2 * FD)[:, :, c1], ALU.add)
                        last = dve.tensor_tensor(w1ho[rows, new, :, c1], w1ho[rows, old, :, c1],
                                                 heads(Y[rows, 0:D], NPAIR, 2 * FD)[:, :, c1], ALU.add)
                    last.then_inc(w_updated, 1)
                elif kind == "Tc1":
                    g = X[:].rearrange("p (h k c) -> p h k c", h=NPAIR, k=2)
                    dve.wait_ge(tq_ready, n + 1)
                    if n >= 1:
                        dve.wait_ge(oi_psum, n)
                    link(dve.scalar_tensor_tensor(heads(sq2[:], NPAIR, P), heads(tq[:], NPAIR, P), 1.0, g[:, :, 0],
                                                  ALU.add, ALU.mult))
                    dve.scalar_tensor_tensor(hqT[:], heads(sq2[:], NPAIR, P), 0.5, g[:, :, 1], ALU.mult, ALU.mult)\
                       .then_inc(hq_ready, 1)
                elif kind == "Tc2":
                    dve.wait_ge(sqo_ready, n + 1)
                    dve.tensor_reduce(ss4[:], heads(sqo[:], NH, FD), AX.X, ALU.add).then_inc(ss4_ready, 1)
                elif kind == "Tc3":
                    dve.wait_ge(r4_ready, n + 1)
                    if n >= 1:
                        dve.wait_ge(yT_psum, n)
                    dve.tensor_tensor(heads(tt[:], NH, FD), heads(Y[:, 0:D], NH, FD), spread(r4[:], NH, FD), ALU.mult)\
                       .then_inc(tt_ready, 1)
                    dve.wait_ge(tt_ready, n + 1)
                    dve.tensor_tensor(heads(ttw[:], NH, FD), heads(tt[:], NH, FD),
                                      ttw_w.unsqueeze(1).broadcast_to([P, NH, FD]), ALU.mult).then_inc(ttw_ready, 1)

        @block.tensor
        def _(pe):
            def wait_all(*pairs):
                for s, v in pairs:
                    pe.wait_ge(s, v)

            pe.wait_ge(l_ident, 16)
            for step in SCHEDULE["pe"]:
                kind, n = step[0], step[1] if len(step) > 1 else 0
                if kind == "C":
                    pe.wait_ge(coef_ready, 1)
                    for t in range(2):
                        mm = pe.transpose(OT[:].bitcast(BF16)[0:3 * E, t * P:(t + 1) * P], coef3[:, t], identb[:])
                    mm.then_inc(coefT_psum, 1)
                elif kind == "CX":
                    if n == 0:
                        pe.wait_ge(coefT_ready, 1)
                        pe.wait_ge(l_expand, 16)
                    if n >= 2:
                        pe.wait_ge(coefx_ready, n - 1)
                    for a in range(2):
                        i = 2 * n + a
                        mm = pe.matmul((SC, PT)[n % 2][:, a * D:(a + 1) * D], expand[:, i * P:(i + 1) * P],
                                       coefT[:], start=True, stop=True)
                    mm.then_inc(coefx_psum, 1)
                elif kind == "G1":
                    pe.wait_ge(fxn_ready, n + 1)
                    if n:
                        pe.wait_ge(gated, n * NU)
                    for k in range(DK):
                        mm = pe.transpose(GU[(n * NU + 1) % 2][:, k * P:(k + 1) * P], fxn[:, k * P:(k + 1) * P], ident[:])
                    mm.then_inc(fxT_psum, 1)
                elif kind == "F":
                    i, t = step[2], n % 2
                    m = n * NU + i
                    if i == 0:
                        pe.wait_ge(fxT_ready, n + 1)
                    if n == 0:
                        pe.wait_ge(l_wff[i], 16)
                    if m >= 2:
                        pe.wait_ge(gated, m - 1)
                    for g in range(2):
                        for a in range(2):
                            for k in range(DK):
                                mm = pe.matmul(GU[m % 2][:, (2 * g + a) * P:(2 * g + a + 1) * P],
                                               wff[:, 2 * i + a, (2 * g + k) * P:(2 * g + k + 1) * P],
                                               fxT[:, t, k * P:(k + 1) * P], start=(k == 0), stop=(k == DK - 1))
                    mm.then_inc(gu_ready, 1)
                elif kind == "D":
                    i = step[2]
                    m = n * NU + i
                    pe.wait_ge(h_ready, m + 1)
                    if i == 0 and n:
                        pe.wait_ge(ffn_added, n)
                    for a in range(2):
                        mm = pe.matmul(DN[:, 0:D], fh[:, m % 3, a * P:(a + 1) * P], wff[:, 2 * i + a, 2 * D:3 * D],
                                       start=(i == 0 and a == 0), stop=(i == NU - 1 and a == 1))
                    mm.then_inc(down_done, 1)
                elif kind == "P1":
                    pe.wait_ge(xn_ready, n + 1)
                    if n >= 2:
                        pe.wait_ge(attn_ready, n - 1)
                    elif n == 1:
                        pe.wait_ge(fvT_ready, 1)
                    for k in range(DK):
                        mm = pe.transpose(X[:, k * P:(k + 1) * P], xn[:, k * P:(k + 1) * P], ident[:])
                    mm.then_inc(xnT_psum, 1)
                elif kind == "P2":
                    pe.wait_ge(xnT_ready, n + 1)
                    if n == 0:
                        pe.wait_ge(l_wqkv, 16)
                    if n >= 2:
                        pe.wait_ge(x2_ready, n - 1)
                        pe.wait_ge(yT_ready, n - 1)
                    elif n == 1:
                        pe.wait_ge(qkT_ready, 1)
                    for k in range(DK):
                        pe.matmul(X[:], xnT[:, k], wqkv[:, k, 0:512], start=(k == 0), stop=(k == DK - 1))
                    for k in range(DK):
                        mm = pe.matmul(Y[:, 0:D + 3 * NH], xnT[:, k], wqkv[:, k, 512:], start=(k == 0),
                                       stop=(k == DK - 1))
                    mm.then_inc(qkv_ready, 1)
                elif kind == "P3":
                    pe.wait_ge(fn_ready, n + 1)
                    if n == 0:
                        pe.wait_ge(qkv_sb, 1)
                    else:
                        pe.wait_ge(hq_ready, n)
                    for j in range(4):
                        mm = pe.transpose(X[:, j * P:(j + 1) * P], fn[:, j * P:(j + 1) * P], ident[:])
                    mm.then_inc(fT_psum, 1)
                elif kind == "PR":
                    pe.wait_ge(rope_ready, n + 1)
                    if n == 0:
                        pe.wait_ge(qkv_sb, 1)
                    else:
                        pe.wait_ge(w_updated, n)
                    for j in range(4):
                        mm = pe.transpose(Y[:, j * P:(j + 1) * P], rope[:, j * P:(j + 1) * P], ident[:])
                    mm.then_inc(qkT_psum, 1)
                elif kind == "P4":
                    pe.wait_ge(fT_ready, n + 1)
                    for j in range(NPAIR):
                        mm = pe.transpose(X[:, j * P:(j + 1) * P], s2v[:, n % 2, j * P:(j + 1) * P],
                                          ident[:])
                    mm.then_inc(fvT_psum, 1)
                elif kind == "S":
                    (b, t), u, s = ORDER[n], step[2], n % 2
                    q = UBASE[n] + u
                    nh = 4 if t == 0 else 2
                    w = 512 // nh
                    if u == 0:
                        pe.wait_ge(qkT_ready, n + 1)
                    if q:
                        pe.wait_ge(nmax_ready, q)
                    else:
                        pe.wait_ge(coefx_ready, FT // 2)
                    for a, h in enumerate(unit_heads(t, u)):
                        c, j, par_ = h // 8, (h % 8) // 2, h % 2
                        rows = slice(32 * j, 32 * j + 32)
                        mm = pe.matmul(SC[:, a * w:(a + 1) * w], qTm[rows, s, par_, c], kT[rows, KV_SLOT[b], c, 0:w],
                                       start=True, stop=True)
                    mm.then_inc(scores_ready, 1)
                elif kind == "T":
                    q = UBASE[n] + step[2]
                    pe.wait_ge(exp_done, q + 1)
                    if q:
                        pe.wait_ge(pT_ready, q)
                    for j in range(4):
                        mm = pe.transpose(PT[:, j * P:(j + 1) * P], pS[:, q % 2, j * P:(j + 1) * P], ident[:])
                    mm.then_inc(pT_psum, 1)
                elif kind == "V":
                    (b, t), u = ORDER[n], step[2]
                    q = UBASE[n] + u
                    pe.wait_ge(pT_ready, q + 1)
                    if u == 0:
                        pe.wait_ge(qkv_sb, n + 1)
                        pe.wait_ge(consts, 1)
                        if n:
                            pe.wait_ge(oS_ready, n)
                    for k in range(t + 1):
                        for a, h in enumerate(unit_heads(t, u)):
                            g, j = h // 4, h % 4
                            mm = pe.matmul(OT[32 * j:32 * j + 32, g * P:(g + 1) * P], vS[:, KV_SLOT[b], k, HD * h:HD * h + 32],
                                           pT[:, q % 2, (a * (t + 1) + k) * P:(a * (t + 1) + k + 1) * P],
                                           start=(k == 0), stop=(k == t))
                    mm.then_inc(pv_done, 1)
                elif kind == "O1":
                    pe.wait_ge(oS_ready, n + 1)
                    if n + 1 < NT:
                        pe.wait_ge(fvT_ready, n + 2)
                    else:
                        pe.wait_ge(hq_ready, n + 1)
                    for j in range(4):
                        mm = pe.transpose(X[:, j * P:(j + 1) * P], oS[:, j * P:(j + 1) * P], ident[:])
                    mm.then_inc(o_psum, 1)
                elif kind == "O2":
                    pe.wait_ge(y_ready, n + 1)
                    for k in range(DK):
                        mm = pe.transpose(Y[:, k * P:(k + 1) * P], yS[:, k * P:(k + 1) * P], ident[:])
                    mm.then_inc(yT_psum, 1)
                elif kind == "O3":
                    pe.wait_ge(yT_ready, n + 1)
                    if n + 2 < NT:
                        pe.wait_ge(xnT_ready, n + 3)
                    else:
                        pe.wait_ge(attn_ready, n + 1)
                    if n == 0:
                        pe.wait_ge(l_wo, 16)
                    for k in range(DK):
                        mm = pe.matmul(X[:, 0:D], yT[:, k], wo[:, k], start=(k == 0), stop=(k == DK - 1))
                    mm.then_inc(wo_psum, 1)
                elif kind == "Ta":
                    s, old = n % 2, w_old(n)
                    wait_all((fT_ready, n + 1), (fvT_ready, n + 1))
                    if old == INIT:
                        wait_all((l_init, 16 * 3 * NH), (zeroed, 3))
                    else:
                        pe.wait_ge(w_updated, ORDER.index((ORDER[n][0], 0)) + 1)
                    if n + 1 < NT:
                        pe.wait_ge(qkv_sb, n + 2)
                    else:
                        pe.wait_ge(x2_ready, n)
                        pe.wait_ge(yT_ready, n)
                    for p in range(NPAIR):
                        pe.matmul(X[:, p * D:(p + 1) * D], fT[:, 2 + p], w02[:, old, p], start=True, stop=True)
                    for p in range(NPAIR):
                        mm = pe.matmul(Y[:, p * P:(p + 1) * P], fvT[:, p], w1oh[:, old, p], start=True, stop=True)
                    mm.then_inc(ta_psum, 1)
                elif kind == "Tb":
                    s, t = n % 2, ORDER[n][1]
                    pe.wait_ge(dd_ready, n + 1)
                    def blocks(bank, at, left, right):
                        for a in range(2):
                            c = slice(at + FD * a, at + FD * a + FD)
                            mm = pe.matmul(bank[FD * a:FD * a + FD, c], left(a), right(a), start=True, stop=True)
                        return mm
                    for p in range(NPAIR):
                        def of(ap, off):
                            return lambda a: ap[:, off + p * P + FD * a:off + p * P + FD * a + FD]
                        for k in range(2):
                            blocks(X, p * D + k * P, of(fn, D), lambda a: dd[:, p, k, FD * a:FD * a + FD])
                        mm = blocks(Y, p * P, of(hid, 0), of(vl, 0))
                        if t == 0:
                            mm = blocks(Y, D + p * P, of(vl, 0), of(hid, 0))
                    mm.then_inc(tb_psum, 1)
                elif kind == "Tc1":
                    new = KV_SLOT[ORDER[n][0]]
                    pe.wait_ge(w_updated, n + 1)
                    for p in range(NPAIR):
                        for k in range(2):
                            mm = pe.matmul(X[:, p * D + k * P:p * D + (k + 1) * P], w02[:, new, p, k], fT[:, p],
                                           start=True, stop=True)
                    mm.then_inc(gq_psum, 1)
                elif kind == "Tc2":
                    pe.wait_ge(hq_ready, n + 1)
                    if n + 1 < NT:
                        pe.wait_ge(qkT_ready, n + 2)
                    for p in range(NPAIR):
                        mm = pe.matmul(Y[:, p * P:(p + 1) * P], hqT[:, p], w1ho[:, KV_SLOT[ORDER[n][0]], p], start=True, stop=True)
                    mm.then_inc(oi_psum, 1)


def kernel(**inputs):
    import numpy as np
    import concourse.bacc as bacc
    from concourse.bass_utils import run_bass_kernel_spmd

    def get(name):
        return np.asarray(inputs[name])

    f32 = np.float32
    gate = get("L0_ffn_gate_weight").reshape(E * I, D).T.reshape(DK, P, FT, P)
    up = get("L0_ffn_up_weight").reshape(E * I, D).T.reshape(DK, P, FT, P)
    down = get("L0_ffn_down_weight").transpose(0, 2, 1).reshape(FT, P, D)
    wff = np.concatenate([gate[0], gate[1], up[0], up[1], down.transpose(1, 0, 2)], axis=2)
    wqkv = np.concatenate([get("L0_attn_Wqkv"), get("L0_attn_lr_w")], axis=0).T
    wqkv = wqkv.reshape(DK, P, 3 * D + 3 * NH).transpose(1, 0, 2)
    wo = get("L0_attn_Wo").T.reshape(DK, P, D).transpose(1, 0, 2)
    w0, w1, w2 = get("L0_attn_w0"), get("L0_attn_w1"), get("L0_attn_w2")
    w02 = np.stack([w0.transpose(0, 2, 1), w2.transpose(0, 2, 1)], axis=2)
    w1s = np.stack([w1, w1.transpose(0, 2, 1)], axis=1)
    par = np.concatenate([
        get("L0_attn_q_norm_w"), get("L0_attn_k_norm_w"), get("L0_attn_qk_scale").T.reshape(-1),
        get("L0_attn_qk_offset").T.reshape(-1), get("L0_attn_ttt_norm_w"), get("L0_attn_lr_b")])
    idx = get("L0_ffn_topk_idx").reshape(2, P, TOPK).transpose(1, 0, 2)
    topw = get("L0_ffn_topk_weight").reshape(2, P, TOPK).transpose(1, 0, 2)
    inv_freq = (1.0 / f32(500000.0) ** (np.arange(0, HD, 2, dtype=f32) / f32(HD))).astype(f32)
    ang = (np.arange(S, dtype=f32)[:, None] * inv_freq[None, :]).astype(f32)
    cos, sin = np.cos(ang).astype(f32), np.sin(ang).astype(f32)
    trig = np.stack([cos, -sin, sin], axis=1).reshape(2, P, 3, 8).transpose(1, 0, 2, 3).reshape(P, 48)
    part = np.arange(P)
    parity = (part // HD) % 2
    small = np.concatenate([trig, np.stack([parity == 0, parity == 1], 1), np.tile(np.arange(E), (P, 1))], axis=1)
    qi, kj = part[:, None], part[None, :]
    causal = np.where(kj <= qi, 0.0, MASKED)
    before = np.where(kj > qi, 0.0, MASKED)
    mask = np.concatenate([causal, before, causal], axis=1)
    quarter = np.uint16(0x3E80)
    expand = np.tile(quarter * (np.arange(E)[:, None] == (np.arange(E * I) // I)[None, :]), (3, 1)).astype(np.uint16)

    arrays = {
        "x": get("L0_attn_hidden_states"), "wff": wff, "wqkv": wqkv, "wo": wo, "w02": w02, "w1": w1s, "idx": idx,
        "topw": topw, "par": par, "ident": np.eye(P), "mask": mask, "small": small, "expand": expand,
    }
    ints = {"idx", "expand"}
    arrays = {k: np.ascontiguousarray(v if k in ints else v.astype(f32, copy=False)) for k, v in arrays.items()}
    nc = bacc.Bacc("TRN2", target_bir_lowering=False, num_devices=1)
    aps = [nc.dram_tensor(k + "_dram", v.shape, mybir.dt.from_np(v.dtype), kind="ExternalInput").ap() for k, v in arrays.items()]
    aps.append(nc.dram_tensor("out", (B, S, D), F32, kind="ExternalOutput").ap())
    build(nc, *aps)
    r = run_bass_kernel_spmd(nc, [{k + "_dram": v for k, v in arrays.items()}], core_ids=[0])
    return r.results[0]["out"]
```
